# Optimizing a Trainium2 kernel written in Bass

```python
import numpy as np
import jax
import jax.numpy as jnp

def _softmax(x, axis=-1):
    return jax.nn.softmax(x, axis=axis)

def _gelu(x):
    return jax.nn.gelu(x, approximate=True)

def _silu(x):
    return jax.nn.silu(x)

def _sigmoid(x):
    return jax.nn.sigmoid(x)

def _layernorm(x, axis=-1, eps=1e-05):
    m = jnp.mean(x, axis=axis, keepdims=True)
    v = jnp.var(x, axis=axis, keepdims=True)
    return (x - m) / jnp.sqrt(v + eps)

def _scatter_add(tgt, idx, src, axis=0):
    return tgt.at[idx].add(src)

def _segment_sum(src, seg, n):
    return jax.ops.segment_sum(src, seg, n)
kernel_name = 'mk_cond_resid_d2_seqx_r8_1a7272'

def setup_inputs(seed: int=0):
    np.random.seed(seed)
    _w = jnp.asarray

    def _rec_inputs():
        import jax
        import jax.numpy as jnp
        _rk = jax.random.key(seed)
        x = -0.000125 + 0.9999 * jax.random.normal(jax.random.fold_in(_rk, 1), (32, 32, 256), jnp.float32)
        _lenS = 32 - jax.random.randint(jax.random.fold_in(_rk, 7), (32,), 0, max(1, 32 // 4) + 1, jnp.int32)
        _lenS2 = 32 - jax.random.randint(jax.random.fold_in(_rk, 8), (32,), 0, max(1, 32 // 4) + 1, jnp.int32)
        cond_2048 = 0.000782532 + 0.100527 * jax.random.normal(jax.random.fold_in(_rk, 11), (32, 256), jnp.float32)
        return (x, cond_2048)
    x, cond_2048 = _rec_inputs()

    def _L0_cond_setup():
        import jax, jax.numpy as jnp
        import numpy as np
        key = jax.random.key(seed)
        k1, k2 = jax.random.split(key)
        B, T, C, K = (4, 512, 256, 4)
        x = jax.random.normal(k1, (B, T, C), dtype=jnp.float32)
        w = jax.random.normal(k2, (K, 1, C), dtype=jnp.float32) * 0.1
        return {'x': x, 'w': w}
    _L0_cond_all = _L0_cond_setup()
    _L0_cond_in = {k: v for k, v in _L0_cond_all.items() if k in ()}
    del _L0_cond_all

    def _L1_cond_setup():
        import jax, jax.numpy as jnp
        import numpy as np
        DIM = 256
        H = 16
        DH = 128
        INNER = H * DH
        MLP = 4 * DIM
        B, T = (2, 256)
        EPS = 1e-06

        def _ln(x):
            mu = jnp.mean(x, axis=-1, keepdims=True)
            var = jnp.var(x, axis=-1, keepdims=True)
            return (x - mu) * jax.lax.rsqrt(var + EPS)
        key = jax.random.key(seed)
        ks = jax.random.split(key, 12)
        s = 0.02
        return {'x': jax.random.normal(ks[0], (B, T, DIM), jnp.float32), 'timestep_embed': jax.random.normal(ks[1], (B, DIM), jnp.float32), 'ada_w': jax.random.normal(ks[2], (DIM, 6 * DIM), jnp.float32) * s, 'ada_b': jnp.zeros((6 * DIM,), jnp.float32), 'qkv_w': jax.random.normal(ks[3], (DIM, 3 * INNER), jnp.float32) * s, 'qkv_b': jnp.zeros((3 * INNER,), jnp.float32), 'out_w': jax.random.normal(ks[4], (INNER, DIM), jnp.float32) * s, 'out_b': jnp.zeros((DIM,), jnp.float32), 'ffn_w1': jax.random.normal(ks[5], (DIM, MLP), jnp.float32) * s, 'ffn_b1': jnp.zeros((MLP,), jnp.float32), 'ffn_w2': jax.random.normal(ks[6], (MLP, DIM), jnp.float32) * s, 'ffn_b2': jnp.zeros((DIM,), jnp.float32)}
    _L1_cond_all = _L1_cond_setup()
    _L1_cond_in = {k: v for k, v in _L1_cond_all.items() if k in ('ada_w', 'ada_b', 'qkv_w', 'qkv_b', 'out_w', 'out_b', 'ffn_w1', 'ffn_b1', 'ffn_w2', 'ffn_b2')}
    del _L1_cond_all
    return {'x': x, 'cond_2048': cond_2048, 'L1_cond_ada_w': _L1_cond_in['ada_w'], 'L1_cond_ada_b': _L1_cond_in['ada_b'], 'L1_cond_qkv_w': _L1_cond_in['qkv_w'], 'L1_cond_qkv_b': _L1_cond_in['qkv_b'], 'L1_cond_out_w': _L1_cond_in['out_w'], 'L1_cond_out_b': _L1_cond_in['out_b'], 'L1_cond_ffn_w1': _L1_cond_in['ffn_w1'], 'L1_cond_ffn_b1': _L1_cond_in['ffn_b1'], 'L1_cond_ffn_w2': _L1_cond_in['ffn_w2'], 'L1_cond_ffn_b2': _L1_cond_in['ffn_b2']}

def reference(x, cond_2048, L1_cond_ada_w, L1_cond_ada_b, L1_cond_qkv_w, L1_cond_qkv_b, L1_cond_out_w, L1_cond_out_b, L1_cond_ffn_w1, L1_cond_ffn_b1, L1_cond_ffn_w2, L1_cond_ffn_b2):
    import jax
    import jax.numpy as jnp

    def _L0_cond_ref(x, w):
        import jax, jax.numpy as jnp
        import numpy as np
        K = w.shape[0]
        C = x.shape[-1]
        y = jax.lax.conv_general_dilated(x, w, window_strides=(1,), padding=[(K - 1, 0)], dimension_numbers=('NHC', 'HIO', 'NHC'), feature_group_count=C)
        return y

    def _L1_cond_ref(x, timestep_embed, ada_w, ada_b, qkv_w, qkv_b, out_w, out_b, ffn_w1, ffn_b1, ffn_w2, ffn_b2):
        import jax, jax.numpy as jnp
        import numpy as np
        DIM = 256
        H = 16
        DH = 128
        INNER = H * DH
        MLP = 4 * DIM
        B, T = (2, 256)
        EPS = 1e-06

        def _ln(x):
            mu = jnp.mean(x, axis=-1, keepdims=True)
            var = jnp.var(x, axis=-1, keepdims=True)
            return (x - mu) * jax.lax.rsqrt(var + EPS)
        Bc, Tc, D = x.shape
        ada = (timestep_embed @ ada_w + ada_b)[:, None, :]
        shift1, scale1, gate1, shift2, scale2, gate2 = jnp.split(ada, 6, axis=-1)
        x1 = _ln(x) * (1.0 + scale1) + shift1
        qkv = (x1 @ qkv_w + qkv_b).reshape(Bc, Tc, 3, H, DH)
        q, k, v = (qkv[:, :, 0], qkv[:, :, 1], qkv[:, :, 2])
        scale = DH ** (-0.5)
        attn = jnp.einsum('bthd,bshd->bhts', q, k) * scale
        attn = jax.nn.softmax(attn, axis=-1)
        attn_out = jnp.einsum('bhts,bshd->bthd', attn, v).reshape(Bc, Tc, INNER)
        attn_out = attn_out @ out_w + out_b
        x = x + gate1 * attn_out
        x2 = _ln(x) * (1.0 + scale2) + shift2
        h = jax.nn.gelu(x2 @ ffn_w1 + ffn_b1, approximate=False)
        x = x + gate2 * (h @ ffn_w2 + ffn_b2)
        return x
    x = x + _L0_cond_ref(x, cond_2048[:, None, :])
    x = x + _L1_cond_ref(x, cond_2048, L1_cond_ada_w, L1_cond_ada_b, L1_cond_qkv_w, L1_cond_qkv_b, L1_cond_out_w, L1_cond_out_b, L1_cond_ffn_w1, L1_cond_ffn_b1, L1_cond_ffn_w2, L1_cond_ffn_b2)
    return x

_drawn_inputs = setup_inputs


def setup_inputs(seed=0):
    import zlib

    import numpy as np

    out = dict(_drawn_inputs(seed))
    spreads = {'L1_cond_ada_b': (0.0, 0.8),
     'L1_cond_qkv_b': (0.0, 0.8),
     'L1_cond_out_b': (0.0, 2.0),
     'L1_cond_ffn_b1': (0.0, 0.8),
     'L1_cond_ffn_b2': (0.0, 2.0)}
    factors = {'L1_cond_ada_w': 8.0,
     'L1_cond_qkv_w': 8.0,
     'L1_cond_out_w': 8.0,
     'L1_cond_ffn_w1': 8.0,
     'L1_cond_ffn_w2': 8.0}
    for name, (base, spread) in spreads.items():
        noise = np.random.default_rng([zlib.crc32(name.encode()), seed]).standard_normal(out[name].shape)
        drawn = base * np.exp(spread * noise) if base else spread * noise
        out[name] = jnp.asarray(drawn.astype(out[name].dtype))
    for name, factor in factors.items():
        out[name] = (out[name] * factor).astype(out[name].dtype)
    return out
```

```python
from contextlib import ExitStack

import concourse.bass as bass
from concourse import mybir

F32 = mybir.dt.float32
F32R = mybir.dt.float32r
ALU = mybir.AluOpType
ACT = mybir.ActivationFunctionType
AX_X = mybir.AxisListType.X

P = 128
HALVES = 2
EPS = 1e-6


def cond_resid_block_kernel(nc, x, cond, ada_w, ada_b, qkv_w, qkv_b, out_w, out_b,
                            ffn_w1, ffn_b1, ffn_w2, ffn_b2, out):
    B, T, C = x.shape
    TOK = B * T
    CT = C // P
    INNER = out_w.shape[0]
    NH = INNER // P
    GH = 4
    NG = NH // GH
    HT = TOK // HALVES
    HB = B // HALVES
    TG = HT // P
    QB = P // T
    MLP = ffn_w1.shape[1]
    MT = MLP // P
    ADA = ada_w.shape[1] // P
    SCALE = float(P) ** -0.5
    PIECE = 512
    UNIT_BANKS = 2 * GH + TG
    assert T == 32 and HT == PIECE and GH * P == PIECE and CT == 2 and MT == 8

    B_QKV, B_ADA = 0, 3 * NH
    B_OUT = B_ADA + ADA
    B_F1 = B_OUT + CT
    B_F2 = B_F1 + MT
    NBIAS = B_F2 + CT
    SHIFT1, SCALE1, GATE1, SHIFT2, SCALE2, GATE2 = range(6)
    DVE_LAGS = list(range(1, 13))
    PE_LAGS = [0] + list(range(13, T))
    ND = len(PE_LAGS) * CT
    DVE_CONV_OPS = CT * (len(DVE_LAGS) + 1)

    with ExitStack() as ctx:
        def sb(name, shape, dt=F32):
            return ctx.enter_context(nc.sbuf_tensor(name, shape, dt))

        def sem(name):
            return ctx.enter_context(nc.semaphore(name))

        x0 = sb("x0", [P, CT, TOK])
        xc = sb("xc", [P, CT, TOK])
        x1h = sb("x1h", [P, CT, TOK], F32R)
        x1l = sb("x1l", [P, CT, TOK], F32R)
        yacc = sb("yacc", [P, CT, TOK])
        raw = sb("raw", [P, 8 * PIECE])
        wh = sb("wh", [P, 8 * PIECE], F32R)
        wl = sb("wl", [P, 8 * PIECE], F32R)
        pool = sb("pool", [P, 16 * PIECE])
        pt = sb("pt", [P, HALVES, TG, GH, P])
        oh = sb("oh", [P, GH, HT], F32R)
        ol = sb("ol", [P, GH, HT], F32R)
        sd = sb("sd", [P, PIECE])
        pe_ = sb("pexp", [P, PIECE])
        pn = sb("pnorm", [P, PIECE])
        hh = sb("hh", [P, MT, HT], F32R)
        hl = sb("hl", [P, MT, HT], F32R)
        adaw = sb("adaw", [P, CT, ada_w.shape[1]])
        ident = sb("ident", [P, P])
        ones = sb("ones", [P, P])
        rows = sb("rows", [NBIAS, P])
        crow = sb("crow", [B, C])
        bT = sb("bT", [P, NBIAS])
        condT = sb("condT", [P, CT, B])
        adaT = sb("adaT", [P, ADA, B])
        bg = sb("bg", [P, 3, GH])
        mx = sb("mx", [P, GH * TG])
        sm = sb("sm", [P, GH * TG])
        rc = sb("rc", [P, GH * TG])
        ve = sb("ve", [P, TG])
        rs = sb("rs", [P, TG])
        mhalf = sb("mhalf", [P, TG])

        q_sb = pool[:, 0:2048].rearrange("p (h t) -> p h t", h=GH)
        k_sb = pool[:, 2048:4096].rearrange("p (h t) -> p h t", h=GH)
        v_sb = pool[:, 4096:8192].rearrange("p (s g n) -> p s g n", s=HALVES, g=TG)
        diag = pool[:, 0:ND * P].rearrange("p (n c) -> p n c", c=P)
        xtok = pool[:, 6144:8192].rearrange("p (n c) -> p n c", c=C)
        hf = q_sb
        sq2 = k_sb
        otok = v_sb

        banks = [ctx.enter_context(nc.psum_tensor(f"bank{i}", [P, 512], F32)) for i in range(8)]
        PB, S_BANK, OB, YB = banks[0:3], banks[3], banks[4:6], banks[6:8]

        s_xin, s_row, s_adaw = sem("x_loaded"), sem("rows_loaded"), sem("adaw_loaded")
        s_xinb = sem("x_loaded_second")
        s_raw = [sem(f"raw_{n}_loaded") for n in ("q", "k", "v", "o")]
        s_const, s_id0, s_zero = sem("constants_set"), sem("ident_zeroed"), sem("pt_zeroed")
        s_bt, s_btc = sem("biases_transposed"), sem("biases_copied")
        s_bgfree, s_bg = sem("group_biases_free"), sem("group_biases_copied")
        s_xt, s_xe, s_xeb = sem("x_transposed"), sem("x_copied"), sem("x_copied_second")
        s_diag, s_cpe, s_cdve = sem("diagonals_built"), sem("conv_pe_done"), sem("conv_dve_steps")
        s_adap, s_adat = sem("ada_product"), sem("ada_steps")
        s_in, s_mean, s_xm, s_sq = sem("ln_input"), sem("ln_mean"), sem("ln_centred"), sem("ln_squares")
        s_var, s_ve, s_rs, s_rb = sem("ln_var"), sem("ln_var_eps"), sem("ln_rstd"), sem("ln_rstd_spread")
        s_mod, s_x1f, s_hi, s_lo = sem("ln_steps"), sem("x1_full"), sem("x1_high"), sem("x1_low")
        s_whi, s_wlo = sem("weights_high"), sem("weights_low")
        s_proj, s_ev = sem("projections"), sem("projections_copied")
        s_s, s_mx, s_sd, s_e = sem("scores"), sem("score_max"), sem("scores_less_max"), sem("exps")
        s_sum, s_rc, s_pn, s_pt = sem("exp_sums"), sem("sum_recips"), sem("probs"), sem("probs_transposed")
        s_pv, s_ohi, s_olo = sem("attn_out"), sem("attn_out_high"), sem("attn_out_low")
        s_y, s_ya = sem("out_proj"), sem("out_proj_added")
        s_res = sem("residual_steps")
        s_f1, s_hf, s_hhi, s_hlo = sem("ffn_hidden"), sem("gelu_done"), sem("hidden_high"), sem("hidden_low")
        s_f2, s_fin, s_ft, s_fe = sem("ffn_out"), sem("result_steps"), sem("result_transposed"), (sem("result_copied_v"), sem("result_copied_a"))
        s_out = sem("stored")

        def half(t, ct, n):
            return t[:, ct, n * HT:(n + 1) * HT]

        def by_batch(ap):
            return ap.rearrange("p (b t) -> p b t", t=T)

        def ada(chunk, ct, n):
            v = adaT[:, CT * chunk + ct, n * HB:(n + 1) * HB]
            return v.unsqueeze(2).to_broadcast([P, HB, T])

        def ln_in(n, ct):
            return half(xc, ct, n) if n < 2 else half(yacc, ct, n - 2)

        def ln_c(n, ct):
            return half(yacc, ct, n) if n < 2 else half(x0, ct, n - 2)

        def ln_sq(n, ct):
            return half(x0, ct, n) if n < 2 else sq2[:, CT * (n - 2) + ct, :]

        LN_BANK = [YB[0], YB[0], PB[0], OB[0]]

        x_v = x.rearrange("(n q) t c -> (q t) n c", q=QB)
        out_v = out.rearrange("(n q) t c -> (q t) n c", q=QB)
        qkv_v = qkv_w.rearrange("(k p) n -> p k n", p=P)

        block = ctx.enter_context(nc.Block())

        @block.sync
        def _(sp):
            sp.dma_start(crow[:, :], cond).then_inc(s_row, 16)
            sp.dma_start(xtok[:, 0:TG, :], x_v[:, 0:TG, :]).then_inc(s_xin, 16)
            for at, src in ((B_QKV, qkv_b), (B_ADA, ada_b), (B_OUT, out_b), (B_F1, ffn_b1), (B_F2, ffn_b2)):
                n = src.shape[0] // P
                sp.dma_start(rows[at:at + n, :], src.rearrange("(n p) -> n p", p=P)).then_inc(s_row, 16)
            sp.dma_start(xtok[:, TG:2 * TG, :], x_v[:, TG:2 * TG, :]).then_inc(s_xinb, 16)
            sp.dma_start(adaw[:, :, :], ada_w.rearrange("(k p) n -> p k n", p=P)).then_inc(s_adaw, 16)

            def load_group(hg):
                for i in range(3):
                    if not isinstance(hg, int):
                        sp.wait_ge(s_wlo, hg * 8 - 8 + 2 * i + 2)
                    sp.dma_start(raw[:, 1024 * i:1024 * (i + 1)].rearrange("p (k n) -> p k n", k=CT),
                                 qkv_v[:, :, bass.ds(hg * PIECE + i * INNER, PIECE)]).then_inc(s_raw[i], 16)
                if not isinstance(hg, int):
                    sp.wait_ge(s_wlo, hg * 8)
                sp.dma_start(raw[:, 3072:4096].rearrange("p (h n) -> p h n", h=GH),
                             out_w[bass.ds(hg * PIECE, PIECE), :].rearrange("(h p) n -> p h n", p=P))\
                    .then_inc(s_raw[3], 16)

            load_group(0)
            with sp.Fori(1, NG) as hg:
                load_group(hg)
            w1_v = ffn_w1.rearrange("(k p) n -> p k n", p=P)
            w2_v = ffn_w2.rearrange("(k p) n -> p k n", p=P)
            for i in range(4):
                sp.wait_ge(s_wlo, 8 * (NG - 1) + 2 * i + 2)
                dst = raw[:, 1024 * i:1024 * (i + 1)]
                if i < 2:
                    sp.dma_start(dst, w1_v[:, i, :]).then_inc(s_raw[i], 16)
                else:
                    sp.dma_start(dst.rearrange("p (k n) -> p k n", k=4), w2_v[:, 4 * (i - 2):4 * (i - 1), :])\
                        .then_inc(s_raw[i], 16)
            for n in range(2 * HALVES):
                sp.wait_ge(s_fe[n % 2], n // 2 + 1)
                sp.dma_start(out_v[:, 2 * n:2 * n + 2, :],
                             otok[:, 0, n, :].rearrange("p (m c) -> p m c", c=C)).then_inc(s_out, 16)
            sp.wait_ge(s_out, 16 * 2 * HALVES)

        @block.gpsimd
        def _(g):
            g.memset(ident[:, :], 0.0).then_inc(s_id0, 1)
            g.wait_ge(s_id0, 1)
            g.affine_select(out=ident[:, :], in_=ident[:, :], compare_op=ALU.not_equal, fill=1.0,
                            base=0, pattern=[[-1, P]], channel_multiplier=1).then_inc(s_const, 1)
            g.memset(ones[:, :], 1.0 / C).then_inc(s_const, 1)
            g.memset(mhalf[:, :], -0.5).then_inc(s_const, 1)
            g.wait_ge(s_const, 3)
            g.memset(pt[:, :, :, :, :], 0.0).then_inc(s_zero, 1)

            def low_parts(hg, pieces):
                for p in pieces:
                    cols = slice(PIECE * p, PIECE * (p + 1))
                    g.wait_ge(s_whi, hg * 8 + (p + 1))
                    g.tensor_tensor(wl[:, cols], raw[:, cols], wh[:, cols].bitcast(F32), ALU.subtract)\
                        .then_inc(s_wlo, 1)

            def rstd(n):
                g.wait_ge(s_ve, n + 1)
                g.tensor_tensor(rs[:, :], ve[:, :], mhalf[:, :], ALU.pow).then_inc(s_rs, 1)

            low_parts(0, range(0, 4))
            rstd(0)
            low_parts(0, range(4, 6))
            rstd(1)
            low_parts(0, range(6, 8))
            low_parts(1, range(0, 6))
            with g.Fori(1, NG) as hg:
                low_parts(hg, range(6, 8))
                low_parts(hg + 1, range(0, 6))
            rstd(2)
            low_parts(NG, range(6, 8))

            def hidden_low(n, m):
                g.wait_ge(s_hhi, MT * n + m + 1)
                g.tensor_tensor(hl[:, m, :], hf[:, m % 4, :], hh[:, m, :].bitcast(F32), ALU.subtract)\
                    .then_inc(s_hlo, 1)

            for m in range(4):
                hidden_low(0, m)
            rstd(3)
            for m in range(4, MT):
                hidden_low(0, m)
            for m in range(MT):
                hidden_low(1, m)

        @block.scalar
        def _(a):
            def high_parts(hg, pieces):
                first = isinstance(hg, int) and hg == 0
                for p in pieces:
                    cols = slice(PIECE * p, PIECE * (p + 1))
                    if p % 2 == 0:
                        a.wait_ge(s_raw[p // 2], hg * 16 + 16)
                        if not first:
                            if p < 6:
                                a.wait_ge(s_proj, hg * 24 - 8 + 4 * (p // 2))
                            else:
                                a.wait_ge(s_y, hg * 4)
                    a.activation(wh[:, cols], raw[:, cols], ACT.Copy).then_inc(s_whi, 1)

            a.wait_ge(s_bt, 1)
            a.activation(condT[:, :, :], S_BANK[:, 128:128 + CT * B].rearrange("p (k b) -> p k b", k=CT),
                         ACT.Copy).then_inc(s_btc, 1)
            a.wait_ge(s_const, 1)
            a.wait_ge(s_btc, 1)
            for n in range(ND):
                j, ct = PE_LAGS[n // CT], n % CT
                a.activation(diag[:, n, :], ident[:, :], ACT.Copy,
                             scale=condT[:, ct, T - 1 - j:T - j]).then_inc(s_diag, 1)
                if n in (7, 9):
                    cb = (n - 7) // 2
                    a.wait_ge(s_xt, 3 + cb)
                    a.activation(half(x0, cb, 1), YB[cb][:, :], ACT.Copy).then_inc(s_xeb, 1)
                if n == 11:
                    a.wait_ge(s_bt, 2)
                    a.activation(bT[:, :], PB[2][:, 0:NBIAS], ACT.Copy).then_inc(s_btc, 1)
            high_parts(0, range(0, 4))

            def squares(n):
                for ct in range(CT):
                    a.wait_ge(s_xm, CT * n + ct + 1)
                    a.activation(ln_sq(n, ct), ln_c(n, ct), ACT.Square).then_inc(s_sq, 1)

            def x1_high(n):
                for ct in range(CT):
                    a.wait_ge(s_x1f, CT * n + ct + 1)
                    a.activation(half(x1h, ct, n % 2), ln_c(n, ct), ACT.Copy).then_inc(s_hi, 1)

            squares(0)
            high_parts(0, range(4, 6))
            x1_high(0)

            def evac(hg, u, j):
                a.wait_ge(s_proj, hg * 24 + (12 * u + j + 1))
                src = PB[j % 3][:, :]
                if j < 2 * GH:
                    dst = (q_sb if j < GH else k_sb)[:, j % GH, :]
                    a.activation(dst, src, ACT.Identity, bias=bg[:, j // GH, j % GH:j % GH + 1])\
                        .then_inc(s_ev, 1)
                else:
                    a.activation(v_sb[:, u, j - 2 * GH, :], src, ACT.Copy).then_inc(s_ev, 1)

            def exps(hg, back, units):
                a.wait_ge(s_sd, hg * 2 + (units + 1))
                a.activation(pe_[:, :], sd[:, :], ACT.Exp, scale=SCALE).then_inc(s_e, 1)

            def o_high(hg, prev):
                for h in range(GH):
                    a.wait_ge(s_pv, hg * 8 + (4 * prev + h + 1))
                    a.activation(oh[:, h, :], OB[h % 2][:, :], ACT.Identity,
                                 bias=bg[:, 2, h:h + 1]).then_inc(s_ohi, 1)

            def group_biases(hg, part, width):
                if not isinstance(hg, int):
                    if part == 0:
                        a.wait_ge(s_ev, hg * 24)
                    else:
                        a.wait_ge(s_ohi, hg * 8)
                    a.sem_inc(s_bgfree, 1)
                src = bT[:, B_QKV:B_QKV + 3 * NH].rearrange("p (w g h) -> p w g h", w=3, g=NG)
                a.activation(bg[:, part:part + width, :], src[:, part:part + width, bass.ds(hg, 1), :]
                             .rearrange("p w g h -> p w (g h)"), ACT.Copy).then_inc(s_bg, 1)

            def body(hg, first):
                group_biases(hg, 0, 2)
                a.wait_ge(s_bg, hg * 2 + 1)
                for j in range(UNIT_BANKS):
                    evac(hg, 0, j)
                    if j == 1 and not first:
                        exps(hg, None, -1)
                    if first and j == 7:
                        squares(1)
                if first:
                    x1_high(1)
                if not first:
                    o_high(hg, -1)
                group_biases(hg, 2, 1)
                a.wait_ge(s_bg, hg * 2 + 2)
                for j in range(UNIT_BANKS):
                    evac(hg, 1, j)
                    if j == 1:
                        exps(hg, None, 0)
                    if j == 2:
                        high_parts(hg, range(6, 8))
                    if j == 5:
                        high_parts(hg + 1, range(0, 2))
                    if j == 9:
                        high_parts(hg + 1, range(2, 4))
                high_parts(hg + 1, range(4, 6))
                o_high(hg, 0)

            a.wait_ge(s_btc, 2)
            body(0, True)
            with a.Fori(1, NG) as hg:
                body(hg, False)
            exps(NG - 1, None, 1)
            o_high_last = NG - 1
            for h in range(GH):
                a.wait_ge(s_pv, o_high_last * 8 + 4 + h + 1)
                a.activation(oh[:, h, :], OB[h % 2][:, :], ACT.Identity,
                             bias=bg[:, 2, h:h + 1])\
                    .then_inc(s_ohi, 1)
                if h == 1:
                    squares(2)
            high_parts(NG, range(6, 8))
            x1_high(2)

            def hidden(n, m):
                a.wait_ge(s_f1, MT * n + m + 1)
                if MT * n + m >= 4:
                    a.wait_ge(s_hlo, MT * n + m - 3)
                a.activation(hf[:, m % 4, :], PB[m % 3][:, :], ACT.Gelu,
                             bias=bT[:, B_F1 + m:B_F1 + m + 1]).then_inc(s_hf, 1)
                a.wait_ge(s_hf, MT * n + m + 1)
                a.activation(hh[:, m, :], hf[:, m % 4, :], ACT.Copy).then_inc(s_hhi, 1)

            for m in range(MT):
                hidden(0, m)
                if m == 2:
                    squares(3)
            x1_high(3)
            for m in range(MT):
                hidden(1, m)
            for n in range(1, 2 * HALVES, 2):
                a.wait_ge(s_ft, n + 1)
                a.activation(otok[:, 0, n, :], OB[1][:, :], ACT.Copy).then_inc(s_fe[1], 1)

        @block.vector
        def _(v):
            for ct in range(CT):
                v.wait_ge(s_xt, ct + 1)
                v.tensor_copy(half(x0, ct, 0), OB[ct][:, :]).then_inc(s_xe, 1)

            def conv(n):
                base = n * DVE_CONV_OPS
                step = 0
                for j in DVE_LAGS:
                    for ct in range(CT):
                        xs = by_batch(half(x0, ct, n))
                        acc = by_batch(half(xc, ct, n))
                        w = condT[:, ct, T - 1 - j:T - j]
                        if j == 1:
                            v.scalar_tensor_tensor(out=acc[:, :, 1:], in0=xs[:, :, :T - 1], scalar=w,
                                                   in1=xs[:, :, 1:], op0=ALU.mult, op1=ALU.add).then_inc(s_cdve, 1)
                            v.tensor_copy(acc[:, :, 0:1], xs[:, :, 0:1]).then_inc(s_cdve, 1)
                            step += 2
                            continue
                        v.wait_ge(s_cdve, base + (step - 1 if j > 2 else 2 * (ct + 1)))
                        v.scalar_tensor_tensor(out=acc[:, :, j:], in0=xs[:, :, :T - j], scalar=w,
                                               in1=acc[:, :, j:], op0=ALU.mult, op1=ALU.add).then_inc(s_cdve, 1)
                        step += 1
                for ct in range(CT):
                    v.wait_ge(s_cdve, base + step)
                    v.wait_ge(s_cpe, CT * n + ct + 1)
                    src = (PB if n == 0 else OB)[ct][:, :]
                    v.tensor_tensor(half(xc, ct, n), half(xc, ct, n), src, ALU.add).then_inc(s_in, 1)

            def centre(n):
                v.wait_ge(s_mean, n + 1)
                v.wait_ge(s_in, CT * (n + 1))
                for ct in range(CT):
                    v.tensor_tensor(ln_c(n, ct), ln_in(n, ct), LN_BANK[n][:, :], ALU.subtract)\
                        .then_inc(s_xm, 1)

            def var_eps(n):
                v.wait_ge(s_var, n + 1)
                v.tensor_scalar(ve[:, :], LN_BANK[n][:, 0:TG], EPS, None, ALU.add).then_inc(s_ve, 1)

            def modulate(n):
                shift, scale = (SHIFT1, SCALE1) if n < 2 else (SHIFT2, SCALE2)
                hn = n % 2
                v.wait_ge(s_rb, n + 1)
                v.wait_ge(s_sq, CT * (n + 1))
                for ct in range(CT):
                    v.tensor_tensor(ln_c(n, ct), ln_c(n, ct), LN_BANK[n][:, :], ALU.mult).then_inc(s_mod, 1)
                for ct in range(CT):
                    v.wait_ge(s_mod, 4 * n + ct + 1)
                    c = by_batch(ln_c(n, ct))
                    v.tensor_tensor(c, c, ada(scale, ct, hn), ALU.mult).then_inc(s_mod, 1)
                for ct in range(CT):
                    v.wait_ge(s_mod, 4 * n + ct + 3)
                    c = by_batch(ln_c(n, ct))
                    v.tensor_tensor(c, c, ada(shift, ct, hn), ALU.add).then_inc(s_x1f, 1)
                for ct in range(CT):
                    v.wait_ge(s_hi, CT * n + ct + 1)
                    v.tensor_tensor(half(x1l, ct, hn), ln_c(n, ct), half(x1h, ct, hn).bitcast(F32),
                                    ALU.subtract).then_inc(s_lo, 1)

            v.wait_ge(s_btc, 1)
            v.wait_ge(s_xe, CT)
            conv(0)
            centre(0)
            v.wait_ge(s_adap, 1)
            v.wait_ge(s_btc, 2)
            v.tensor_tensor(adaT[:, :, :], PB[2][:, 0:ADA * B].rearrange("p (m b) -> p m b", b=B),
                            bT[:, B_ADA:B_ADA + ADA].unsqueeze(2).to_broadcast([P, ADA, B]),
                            ALU.add).then_inc(s_adat, 1)
            v.wait_ge(s_adat, 1)
            for chunk in (SCALE1, SCALE2):
                part = adaT[:, CT * chunk:CT * (chunk + 1), :]
                v.tensor_scalar(part, part, 1.0, None, ALU.add).then_inc(s_adat, 1)
            v.wait_ge(s_adat, 3)
            var_eps(0)
            modulate(0)
            v.wait_ge(s_xeb, CT)
            conv(1)
            centre(1)
            var_eps(1)
            modulate(1)
            v.wait_ge(s_zero, 1)

            def softmax_front(hg, u):
                scores = S_BANK[:, :].rearrange("p (n k) -> p n k", k=T)
                v.wait_ge(s_s, hg * 2 + (u + 1))
                v.tensor_reduce(mx[:, :], scores, AX_X, ALU.max).then_inc(s_mx, 1)
                v.wait_ge(s_mx, hg * 2 + (u + 1))
                v.tensor_tensor(sd[:, :].rearrange("p (n k) -> p n k", k=T), scores,
                                mx[:, :].unsqueeze(2).to_broadcast([P, GH * TG, T]), ALU.subtract)\
                    .then_inc(s_sd, 1)

            def softmax_back(hg, u):
                e3 = pe_[:, :].rearrange("p (n k) -> p n k", k=T)
                v.wait_ge(s_e, hg * 2 + (u + 1))
                v.tensor_reduce(sm[:, :], e3, AX_X, ALU.add).then_inc(s_sum, 1)
                v.wait_ge(s_sum, hg * 2 + (u + 1))
                v.reciprocal(rc[:, :], sm[:, :]).then_inc(s_rc, 1)
                v.wait_ge(s_rc, hg * 2 + (u + 1))
                v.tensor_tensor(pn[:, :].rearrange("p (n k) -> p n k", k=T), e3,
                                rc[:, :].unsqueeze(2).to_broadcast([P, GH * TG, T]), ALU.mult)\
                    .then_inc(s_pn, 1)
                v.wait_ge(s_pn, hg * 2 + (u + 1))
                for b in range(QB):
                    rows_b = slice(T * b, T * (b + 1))
                    dst = pt[rows_b, u, :, :, T * b:T * (b + 1)].rearrange("p g h q -> p (g h) q")
                    v.transpose(dst, pn[rows_b, :].rearrange("p (n k) -> p n k", k=T)).then_inc(s_pt, 1)

            def o_low(hg, prev, h):
                group = hg if prev >= 0 else hg - 1
                v.wait_ge(s_ohi, hg * 8 + (4 * prev + h + 1))
                v.scalar_tensor_tensor(out=ol[:, h, :], in0=OB[h % 2][:, :],
                                       scalar=bT[:, bass.ds(group * GH + (2 * NH + h), 1)],
                                       in1=oh[:, h, :].bitcast(F32), op0=ALU.add, op1=ALU.subtract)\
                    .then_inc(s_olo, 1)

            def add_y(hg, prev, first=False):
                hn = prev % 2
                for ct in range(CT):
                    v.wait_ge(s_y, hg * 4 + (2 * prev + ct + 1))
                    if first:
                        v.tensor_copy(half(yacc, ct, hn), YB[ct][:, :]).then_inc(s_ya, 1)
                    else:
                        v.wait_ge(s_ya, hg * 4 + (2 * prev + ct - 3))
                        v.tensor_tensor(half(yacc, ct, hn), half(yacc, ct, hn), YB[ct][:, :], ALU.add)\
                            .then_inc(s_ya, 1)

            softmax_front(0, 0)
            softmax_back(0, 0)
            for h in range(GH):
                o_low(0, 0, h)
            add_y(0, 0, first=True)
            softmax_front(0, 1)
            softmax_back(0, 1)
            def body(hg, first_b):
                for h in range(GH):
                    o_low(hg, -1, h)
                add_y(hg, -1, first=first_b)
                softmax_front(hg, 0)
                softmax_back(hg, 0)
                for h in range(GH):
                    o_low(hg, 0, h)
                add_y(hg, 0)
                softmax_front(hg, 1)
                softmax_back(hg, 1)

            body(1, True)
            with v.Fori(2, NG) as hg:
                body(hg, False)

            res = [0]

            def residual(n):
                for ct in range(CT):
                    v.wait_ge(s_ya, 2 * (2 * (NG - 1) + n) + ct + 1)
                    y = by_batch(half(yacc, ct, n))
                    v.scalar_tensor_tensor(out=y, in0=y, scalar=bT[:, B_OUT + ct:B_OUT + ct + 1],
                                           in1=ada(GATE1, ct, n), op0=ALU.add, op1=ALU.mult).then_inc(s_res, 1)
                    res[0] += 1
                for ct in range(CT):
                    v.wait_ge(s_res, res[0] - 1 + ct)
                    v.tensor_tensor(half(yacc, ct, n), half(yacc, ct, n), half(xc, ct, n), ALU.add)\
                        .then_inc(s_in, 1)

            def residual_sum(n):
                for ct in range(CT):
                    v.wait_ge(s_in, CT * (n + 2) + ct + 1)
                    v.tensor_tensor(half(xc, ct, n), half(xc, ct, n), half(yacc, ct, n), ALU.add)\
                        .then_inc(s_res, 1)
                    res[0] += 1

            L = NG - 1
            residual(0)
            o_low(L + 1, -1, 0)
            o_low(L + 1, -1, 1)
            centre(2)
            o_low(L + 1, -1, 2)
            o_low(L + 1, -1, 3)
            var_eps(2)
            add_y(L + 1, -1)
            modulate(2)
            residual(1)
            centre(3)
            residual_sum(0)
            residual_sum(1)
            var_eps(3)
            modulate(3)

            def result(n):
                for ct in range(CT):
                    v.wait_ge(s_f2, CT * n + ct + 1)
                    f = by_batch(half(x0, ct, n))
                    v.scalar_tensor_tensor(out=f, in0=by_batch(YB[ct][:, :]),
                                           scalar=bT[:, B_F2 + ct:B_F2 + ct + 1],
                                           in1=ada(GATE2, ct, n), op0=ALU.add, op1=ALU.mult).then_inc(s_fin, 1)
                for ct in range(CT):
                    v.wait_ge(s_fin, 4 * n + ct + 1)
                    v.wait_ge(s_res, res[0])
                    v.tensor_tensor(half(x0, ct, n), half(x0, ct, n), half(xc, ct, n), ALU.add)\
                        .then_inc(s_fin, 1)
                v.wait_ge(s_ft, 2 * n + 1)
                v.tensor_copy(otok[:, 0, 2 * n, :], S_BANK[:, :]).then_inc(s_fe[0], 1)

            result(0)
            result(1)

        @block.tensor
        def _(pe):
            pe.wait_ge(s_const, 1)
            pe.wait_ge(s_row, 16 * 6)
            for ct in range(CT):
                m = pe.transpose(S_BANK[:, 128 + B * ct:128 + B * (ct + 1)], crow[:, ct * P:(ct + 1) * P],
                                 ident[0:B, 0:B])
            m.then_inc(s_bt, 1)
            pe.transpose(PB[2][:, 0:NBIAS], rows[:, :], ident[0:NBIAS, 0:NBIAS]).then_inc(s_bt, 1)

            def x_transposes(n):
                pe.wait_ge(s_xin if n == 0 else s_xinb, 16)
                for ct in range(CT):
                    for t in range(TG):
                        m = pe.transpose((OB if n == 0 else YB)[ct][:, t * P:(t + 1) * P],
                                         xtok[:, n * TG + t, ct * P:(ct + 1) * P], ident[:, :])
                    m.then_inc(s_xt, 1)

            x_transposes(0)
            x_transposes(1)

            def conv(n, bank):
                for i, j in enumerate(PE_LAGS):
                    for ct in range(CT):
                        if n == 0:
                            pe.wait_ge(s_diag, CT * i + ct + 1)
                        xs = by_batch(half(x0, ct, n))
                        dst = by_batch(bank[ct][:, :])
                        m = pe.matmul(dst[:, :, j:], diag[:, CT * i + ct, :], xs[:, :, :T - j],
                                      start=(i == 0), stop=(i == len(PE_LAGS) - 1))
                        if i == len(PE_LAGS) - 1:
                            m.then_inc(s_cpe, 1)

            def mean(n):
                pe.wait_ge(s_const, 2)
                pe.wait_ge(s_in, CT * (n + 1))
                for ct in range(CT):
                    m = pe.matmul(LN_BANK[n][:, :], ones[:, :], ln_in(n, ct), start=(ct == 0), stop=(ct == CT - 1))
                m.then_inc(s_mean, 1)

            def var(n):
                pe.wait_ge(s_sq, CT * (n + 1))
                for t in range(TG):
                    for ct in range(CT):
                        m = pe.matmul(LN_BANK[n][:, t:t + 1], ln_sq(n, ct)[:, t * P:(t + 1) * P], ones[:, 0:1],
                                      start=(ct == 0), stop=(ct == CT - 1))
                m.then_inc(s_var, 1)

            def spread(n):
                pe.wait_ge(s_rs, n + 1)
                for t in range(TG):
                    m = pe.matmul(LN_BANK[n][:, t * P:(t + 1) * P], rs[:, t:t + 1].to_broadcast([P, P]), ident[:, :],
                                  start=True, stop=True)
                m.then_inc(s_rb, 1)

            pe.wait_ge(s_xe, CT)
            conv(0, PB)
            pe.wait_ge(s_adaw, 16)
            pe.wait_ge(s_btc, 2)
            for m_ in range(ADA):
                for kt in range(CT):
                    m = pe.matmul(PB[2][:, m_ * B:(m_ + 1) * B], adaw[:, kt, m_ * P:(m_ + 1) * P],
                                  condT[:, kt, :], start=(kt == 0), stop=(kt == CT - 1))
            m.then_inc(s_adap, 1)
            pe.wait_ge(s_xeb, CT)
            mean(0)
            var(0)
            spread(0)
            conv(1, OB)
            pe.wait_ge(s_adat, 3)

            def three(dst, w_cols, kt_x, start, stop):
                xh_, xl_ = kt_x
                pe.matmul(dst, wl[:, w_cols], xh_, start=start, stop=False)
                pe.matmul(dst, wh[:, w_cols], xl_, start=False, stop=False)
                return pe.matmul(dst, wh[:, w_cols], xh_, start=False, stop=stop)

            def project(hg, u, hooks):
                first = isinstance(hg, int) and hg == 0
                if first:
                    pe.wait_ge(s_lo, CT * (u + 1))
                toks = slice(u * HT, (u + 1) * HT)
                for j in range(UNIT_BANKS):
                    if j % GH == 0:
                        pe.wait_ge(s_wlo, hg * 8 + (2 * (j // GH) + 2))
                    if not (first and u == 0 and j < 3):
                        pe.wait_ge(s_ev, hg * 24 + (12 * u + j - 2))
                    dst = PB[j % 3][:, :]
                    for kt in range(CT):
                        s, e = kt == 0, kt == CT - 1
                        if j < 2 * GH:
                            c0 = 1024 * (j // GH) + PIECE * kt + P * (j % GH)
                            m = three(dst, slice(c0, c0 + P), (x1h[:, kt, toks], x1l[:, kt, toks]), s, e)
                        else:
                            t0 = u * HT + P * (j - 2 * GH)
                            tk = slice(t0, t0 + P)
                            wc = slice(2048 + PIECE * kt, 2048 + PIECE * (kt + 1))
                            pe.matmul(dst, x1l[:, kt, tk], wh[:, wc], start=s, stop=False)
                            pe.matmul(dst, x1h[:, kt, tk], wl[:, wc], start=False, stop=False)
                            m = pe.matmul(dst, x1h[:, kt, tk], wh[:, wc], start=False, stop=e)
                    m.then_inc(s_proj, 1)
                    if j in hooks:
                        hooks[j]()

            def scores(hg, u):
                pe.wait_ge(s_ev, hg * 24 + (12 * u + 2 * GH))
                if not (isinstance(hg, int) and hg == 0 and u == 0):
                    pe.wait_ge(s_sd, hg * 2 + u)
                for h in range(GH):
                    for t in range(TG):
                        for b in range(QB):
                            c = t * P + b * T
                            m = pe.matmul(S_BANK[b * T:(b + 1) * T, (t * GH + h) * T:(t * GH + h + 1) * T],
                                          q_sb[:, h, c:c + T], k_sb[:, h, c:c + T], start=True, stop=True)
                m.then_inc(s_s, 1)

            def attend(hg, prev, h, first=False):
                hn = prev % 2
                if h == 0:
                    pe.wait_ge(s_pt, hg * 8 + (4 * prev + 4))
                    pe.wait_ge(s_ev, hg * 24 + (12 * prev + 12))
                if not (first and h < 2):
                    pe.wait_ge(s_olo, hg * 8 + (4 * prev + h - 1))
                for t in range(TG):
                    m = pe.matmul(OB[h % 2][:, t * P:(t + 1) * P], v_sb[:, hn, t, h * P:(h + 1) * P],
                                  pt[:, hn, t, h, :], start=True, stop=True)
                m.then_inc(s_pv, 1)

            def out_proj(hg, prev, h, first=False):
                pe.wait_ge(s_olo, hg * 8 + (4 * prev + h + 1))
                if h == 0:
                    pe.wait_ge(s_wlo, (hg if prev >= 0 else hg - 1) * 8 + 8)
                    if not first:
                        pe.wait_ge(s_ya, hg * 4 + 2 * prev)
                for ct in range(CT):
                    c0 = 3072 + C * h + P * ct
                    m = three(YB[ct][:, :], slice(c0, c0 + P), (oh[:, h, :], ol[:, h, :]), h == 0, h == GH - 1)
                    if h == GH - 1:
                        m.then_inc(s_y, 1)

            def attend_rest(hg, prev, first=False, hooks={}):
                for i, (f, h) in enumerate(((out_proj, 0), (attend, 2), (out_proj, 1), (attend, 3),
                                            (out_proj, 2), (out_proj, 3))):
                    f(hg, prev, h, first)
                    if i in hooks:
                        hooks[i]()

            project(0, 0, {5: lambda: mean(1), 8: lambda: var(1), 10: lambda: spread(1)})
            scores(0, 0)
            project(0, 1, {})
            attend(0, 0, 0, True)
            attend(0, 0, 1, True)
            scores(0, 1)
            attend_rest(0, 0, True)
            with pe.Fori(1, NG) as hg:
                for u in range(2):
                    project(hg, u, {})
                    attend(hg, u - 1, 0)
                    attend(hg, u - 1, 1)
                    scores(hg, u)
                    attend_rest(hg, u - 1)
            attend(NG, -1, 0)
            attend(NG, -1, 1)
            attend_rest(NG, -1, False, {0: lambda: mean(2), 3: lambda: var(2)})
            spread(2)

            def ffn1(n, hooks):
                pe.wait_ge(s_lo, CT * (n + 3))
                pe.wait_ge(s_wlo, 8 * NG + 4)
                toks = slice(n * HT, (n + 1) * HT)
                for m_ in range(MT):
                    i = MT * n + m_
                    if m_ >= 3 or n:
                        pe.wait_ge(s_hf, MT * n + (m_ - 2 if m_ >= 3 else 0))
                    for kt in range(CT):
                        c0 = MLP * kt + P * m_
                        m = three(PB[m_ % 3][:, :], slice(c0, c0 + P), (x1h[:, kt, toks], x1l[:, kt, toks]),
                                  kt == 0, kt == CT - 1)
                    m.then_inc(s_f1, 1)
                    if m_ in hooks:
                        hooks[m_]()

            def ffn2(n):
                pe.wait_ge(s_wlo, 8 * NG + 8)
                pe.wait_ge(s_ya, 4 * NG)
                if n:
                    pe.wait_ge(s_fin, 4 * n)
                for k in range(MT):
                    pe.wait_ge(s_hlo, MT * n + k + 1)
                    for ct in range(CT):
                        c0 = 2048 + C * k + P * ct
                        m = three(YB[ct][:, :], slice(c0, c0 + P), (hh[:, k, :], hl[:, k, :]),
                                  k == 0, k == MT - 1)
                        if k == MT - 1:
                            m.then_inc(s_f2, 1)

            def result_transposes(n):
                pe.wait_ge(s_fin, 4 * (n + 1))
                for pair, bank in enumerate((S_BANK, OB[1])):
                    if n:
                        pe.wait_ge(s_fe[pair], n)
                    for i in range(2):
                        for ct in range(CT):
                            t = 2 * pair + i
                            m = pe.transpose(bank[:, C * i + P * ct:C * i + P * (ct + 1)],
                                             half(x0, ct, n)[:, t * P:(t + 1) * P], ident[:, :])
                    m.then_inc(s_ft, 1)

            ffn1(0, {2: lambda: mean(3), 4: lambda: var(3), 6: lambda: spread(3)})
            ffn2(0)
            ffn1(1, {})
            result_transposes(0)
            ffn2(1)
            result_transposes(1)


_INS = ['x', 'cond_2048', 'L1_cond_ada_w', 'L1_cond_ada_b', 'L1_cond_qkv_w', 'L1_cond_qkv_b', 'L1_cond_out_w',
        'L1_cond_out_b', 'L1_cond_ffn_w1', 'L1_cond_ffn_b1', 'L1_cond_ffn_w2', 'L1_cond_ffn_b2']
_OUTS = [((32, 32, 256), 'float32')]


def kernel(**inputs):
    import numpy as _np
    import concourse.bacc as _bacc
    from concourse import mybir as _mybir
    from concourse.bass_utils import run_bass_kernel_spmd as _run

    nc = _bacc.Bacc("TRN2", target_bir_lowering=False, num_devices=1)
    arrays, args = {}, []
    for name in _INS:
        a = _np.ascontiguousarray(inputs[name])
        arrays[f"in_{name}_dram"] = a
        args.append(nc.dram_tensor(f"in_{name}_dram", a.shape, _mybir.dt.from_np(a.dtype), kind="ExternalInput").ap())
    for i, (shape, dtype) in enumerate(_OUTS):
        dt = _mybir.dt.from_np(_np.dtype(dtype))
        args.append(nc.dram_tensor(f"out_{i}_dram", shape, dt, kind="ExternalOutput").ap())
    cond_resid_block_kernel(nc, *args)
    r = _run(nc, [arrays], core_ids=[0])
    got = tuple(r.results[0][f"out_{i}_dram"] for i in range(len(_OUTS)))
    return got[0]
```

```python
from contextlib import ExitStack

import concourse.bass as bass
from concourse import mybir

F32 = mybir.dt.float32
F32R = mybir.dt.float32r
ALU = mybir.AluOpType
ACT = mybir.ActivationFunctionType
AX_X = mybir.AxisListType.X

P = 128
HALVES = 2
EPS = 1e-6


def cond_resid_block_kernel(nc, x, cond, ada_w, ada_b, qkv_w, qkv_b, out_w, out_b,
                            ffn_w1, ffn_b1, ffn_w2, ffn_b2, out):
    B, T, C = x.shape
    TOK = B * T
    CT = C // P
    INNER = out_w.shape[0]
    NH = INNER // P
    GH = 4
    NG = NH // GH
    HT = TOK // HALVES
    HB = B // HALVES
    TG = HT // P
    QB = P // T
    MLP = ffn_w1.shape[1]
    MT = MLP // P
    ADA = ada_w.shape[1] // P
    SCALE = float(P) ** -0.5
    PIECE = 512
    UNIT_BANKS = 2 * GH + TG
    assert T == 32 and HT == PIECE and GH * P == PIECE and CT == 2 and MT == 8

    B_QKV, B_ADA = 0, 3 * NH
    B_OUT = B_ADA + ADA
    B_F1 = B_OUT + CT
    B_F2 = B_F1 + MT
    NBIAS = B_F2 + CT
    SHIFT1, SCALE1, GATE1, SHIFT2, SCALE2, GATE2 = range(6)
    ADA1 = 2 * CT
    PE_LAGS = [[0] + list(range(6, 17)), [0] + list(range(3, 18)), [0] + list(range(8, 15))]
    DVE_LAGS = [[j for j in range(1, T) if j not in lags] for lags in PE_LAGS]
    DIAG_LAGS = PE_LAGS[0] + sorted(set(PE_LAGS[1] + PE_LAGS[2]) - set(PE_LAGS[0]))
    ND = len(DIAG_LAGS) * CT
    DVE_STEPS = [sum(CT * (len(d) + 1) for d in DVE_LAGS[:n]) for n in range(4)]
    CHUNKS = [(0, HT // 2), (HT // 2, HT // 2), (HT, HT)]
    NC = len(CHUNKS)
    NORMS = CHUNKS + [(0, HT), (HT, HT)]

    with ExitStack() as ctx:
        def sb(name, shape, dt=F32):
            return ctx.enter_context(nc.sbuf_tensor(name, shape, dt))

        def sem(name):
            return ctx.enter_context(nc.semaphore(name))

        x0 = sb("x0", [P, CT, TOK])
        xc = sb("xc", [P, CT, TOK])
        x1h = sb("x1h", [P, CT, TOK], F32R)
        x1l = sb("x1l", [P, CT, TOK], F32R)
        yacc = sb("yacc", [P, CT, TOK])
        raw = sb("raw", [P, 8 * PIECE])
        wh = sb("wh", [P, 8 * PIECE], F32R)
        wl = sb("wl", [P, 8 * PIECE], F32R)
        pool = sb("pool", [P, 16 * PIECE])
        pt = sb("pt", [P, HALVES, GH, TG, P])
        oh = sb("oh", [P, GH, HT], F32R)
        ol = sb("ol", [P, GH, HT], F32R)
        sd = sb("sd", [P, PIECE])
        pe_ = sb("pexp", [P, PIECE])
        pn = sb("pnorm", [P, PIECE])
        ident = sb("ident", [P, P])
        ones = sb("ones", [P, P])
        rows = sb("rows", [NBIAS, P])
        crow = sb("crow", [B, C])
        bT = sb("bT", [P, NBIAS])
        condT = sb("condT", [P, CT, B])
        adaT = sb("adaT", [P, ADA, B])
        bg = sb("bg", [P, 3, GH])
        mx = sb("mx", [P, GH * TG])
        sm = sb("sm", [P, GH * TG])
        rc = sb("rc", [P, GH * TG])
        ve = sb("ve", [P, TG])
        rs = sb("rs", [P, TG])
        mhalf = sb("mhalf", [P, TG])
        vt = sb("vt", [P, TG, T])
        with nc.sbuf_tensor("diag", [P, ND, P], F32) as diag, \
                nc.sbuf_tensor("adaw", [P, CT, ada_w.shape[1]], F32) as adaw:
            pass
        hh = sb("hh", [P, MT, HT], F32R)
        hl = sb("hl", [P, MT, HT], F32R)

        q_sb = pool[:, 0:2048].rearrange("p (h t) -> p h t", h=GH)
        k_sb = pool[:, 2048:4096].rearrange("p (h t) -> p h t", h=GH)
        v_sb = pool[:, 4096:8192].rearrange("p (s g n) -> p s g n", s=HALVES, g=TG)
        xtok = pool[:, 6144:8192].rearrange("p (n c) -> p n c", c=C)
        hf = q_sb
        sq2 = k_sb
        otok = v_sb

        banks = [ctx.enter_context(nc.psum_tensor(f"bank{i}", [P, 512], F32)) for i in range(8)]
        PB, S_BANK, OB, YB = banks[0:3], banks[3], banks[4:6], banks[6:8]

        s_x = [sem(f"x_chunk{n}_loaded") for n in range(NC)]
        s_row = [sem("cond_loaded"), sem("biases_loaded")]
        s_adaw = [sem("adaw_first_loaded"), sem("adaw_rest_loaded")]
        s_raw = [sem(f"raw_{n}_loaded") for n in ("q", "k", "v", "o")]
        s_const, s_id0, s_zero = sem("constants_set"), sem("ident_zeroed"), sem("pt_zeroed")
        s_condt, s_cond = sem("cond_transposed"), sem("cond_copied")
        s_bt, s_btc = sem("biases_transposed"), sem("biases_copied")
        s_bgfree, s_bg = sem("group_biases_free"), sem("group_biases_copied")
        s_xt = sem("x_transposed")
        s_xe = [sem(f"x_chunk{n}_copied") for n in range(NC)]
        s_diag = [sem("diagonals_by_scalar"), sem("diagonals_by_gpsimd")]
        s_cpe, s_cdve = sem("conv_pe_done"), sem("conv_dve_steps")
        s_adap, s_adat = sem("ada_product"), sem("ada_steps")
        s_in, s_mean, s_xm, s_sq = sem("ln_input"), sem("ln_mean"), sem("ln_centred"), sem("ln_squares")
        s_var, s_ve, s_rs, s_rb = sem("ln_var"), sem("ln_var_eps"), sem("ln_rstd"), sem("ln_rstd_spread")
        s_vt = sem("ln_var_transposed")
        s_sc, s_mod, s_x1f = sem("ln_scaled"), sem("ln_normed"), sem("x1_full")
        s_hi, s_lo = sem("x1_high"), sem("x1_low")
        s_whi, s_wlo = sem("weights_high"), sem("weights_low")
        s_proj, s_ev = sem("projections"), sem("projections_copied")
        s_s, s_mx, s_sd, s_e = sem("scores"), sem("score_max"), sem("scores_less_max"), sem("exps")
        s_sum, s_rc, s_pn, s_pt = sem("exp_sums"), sem("sum_recips"), sem("probs"), sem("probs_transposed")
        s_pv, s_ohi, s_olo = sem("attn_out"), sem("attn_out_high"), sem("attn_out_low")
        s_y, s_ya = sem("out_proj"), sem("out_proj_added")
        s_res, s_xs, s_gt = sem("residual_gated"), sem("residuals_summed"), sem("ffn_gated")
        s_f1, s_hf, s_hhi = sem("ffn_hidden"), sem("gelu_done"), sem("hidden_high")
        s_hlo = (sem("hidden_low_even"), sem("hidden_low_odd"))
        s_f2, s_fin, s_ft = sem("ffn_out"), sem("result_ready"), sem("result_transposed")
        s_fe = (sem("result_copied_v"), sem("result_copied_a"))
        s_out = sem("stored")

        def part(t, ct, span):
            return t[:, ct, span[0]:span[0] + span[1]]

        def half(t, ct, n):
            return part(t, ct, (n * HT, HT))

        def by_batch(ap):
            return ap.rearrange("p (b t) -> p b t", t=T)

        def ada(chunk, ct, span):
            b0, nb = span[0] // T, span[1] // T
            return adaT[:, CT * chunk + ct, b0:b0 + nb].unsqueeze(2).to_broadcast([P, nb, T])

        def ln_in(n, ct):
            return part(xc if n < NC else yacc, ct, NORMS[n])

        def ln_c(n, ct):
            return part(yacc if n < NC else x0, ct, NORMS[n])

        def ln_sq(n, ct):
            if n < NC:
                return part(x0, ct, NORMS[n])
            return half(x0, ct, 1) if n == NC else sq2[:, ct, :]

        CONV_BANKS = [PB[0:2], YB, YB]
        STAT_BANK = [S_BANK, S_BANK, S_BANK, YB[0], OB[0]]
        RSTD_BANK = [S_BANK, S_BANK, S_BANK, S_BANK, OB[0]]

        ADA_PARTS = [(0, ADA1), (ADA1, 2 * ADA1), (2 * ADA1, ADA)]
        ADA_BANKS = [PB[2], PB[0], PB[1]]
        ADA_STEPS = [1, 3, 4]

        ALL, FRONT, BACK = slice(0, HT), slice(0, HT // 2), slice(HT // 2, HT)
        FFN2_PIECES = [(0, 0, YB[0][:, ALL], ALL), (0, 1, YB[1][:, ALL], ALL), (1, 0, YB[0][:, ALL], ALL),
                       (1, 1, YB[1][:, FRONT], FRONT), (1, 1, PB[0][:, FRONT], BACK)]

        x_v = x.rearrange("(n q) t c -> (q t) n c", q=QB)
        out_v = out.rearrange("(n q) t c -> (q t) n c", q=QB)
        qkv_v = qkv_w.rearrange("(k p) n -> p k n", p=P)

        block = ctx.enter_context(nc.Block())

        @block.sync
        def _(sp):
            def load_x(n):
                t0, nt = CHUNKS[n][0] // P, CHUNKS[n][1] // P
                sp.dma_start(xtok[:, t0:t0 + nt, :], x_v[:, t0:t0 + nt, :]).then_inc(s_x[n], 16)

            def load_adaw(i, c0, c1):
                sp.dma_start(adaw[:, :, c0:c1], ada_w.rearrange("(k p) n -> p k n", p=P)[:, :, c0:c1])\
                    .then_inc(s_adaw[i], 16)

            def load_group(hg):
                for i in range(3):
                    if not isinstance(hg, int):
                        sp.wait_ge(s_wlo, hg * 8 - 8 + 2 * i + 2)
                    sp.dma_start(raw[:, 1024 * i:1024 * (i + 1)].rearrange("p (k n) -> p k n", k=CT),
                                 qkv_v[:, :, bass.ds(hg * PIECE + i * INNER, PIECE)]).then_inc(s_raw[i], 16)
                if not isinstance(hg, int):
                    sp.wait_ge(s_wlo, hg * 8)
                sp.dma_start(raw[:, 3072:4096].rearrange("p (h n) -> p h n", h=GH),
                             out_w[bass.ds(hg * PIECE, PIECE), :].rearrange("(h p) n -> p h n", p=P))\
                    .then_inc(s_raw[3], 16)

            load_x(0)
            load_x(1)
            load_adaw(0, 0, ADA1 * P)
            load_x(2)
            for at, src in ((B_QKV, qkv_b), (B_ADA, ada_b), (B_OUT, out_b), (B_F1, ffn_b1), (B_F2, ffn_b2)):
                n = src.shape[0] // P
                sp.dma_start(rows[at:at + n, :], src.rearrange("(n p) -> n p", p=P)).then_inc(s_row[1], 16)
            load_group(0)
            load_adaw(1, ADA1 * P, ADA * P)
            with sp.Fori(1, NG) as hg:
                load_group(hg)
            w1_v = ffn_w1.rearrange("(k p) n -> p k n", p=P)
            w2_v = ffn_w2.rearrange("(k p) n -> p k n", p=P)
            for i in range(4):
                sp.wait_ge(s_wlo, 8 * (NG - 1) + 2 * i + 2)
                dst = raw[:, 1024 * i:1024 * (i + 1)]
                if i < 2:
                    sp.dma_start(dst, w1_v[:, i, :]).then_inc(s_raw[i], 16)
                else:
                    sp.dma_start(dst.rearrange("p (k n) -> p k n", k=4), w2_v[:, 4 * (i - 2):4 * (i - 1), :])\
                        .then_inc(s_raw[i], 16)
            for n in range(2 * HALVES):
                sp.wait_ge(s_fe[n % 2], n // 2 + 1)
                sp.dma_start(out_v[:, 2 * n:2 * n + 2, :],
                             otok[:, 0, n, :].rearrange("p (m c) -> p m c", c=C)).then_inc(s_out, 16)
            sp.wait_ge(s_out, 16 * 2 * HALVES)

        @block.gpsimd
        def _(g):
            g.memset(ident[:, :], 0.0).then_inc(s_id0, 1)
            g.wait_ge(s_id0, 1)
            g.affine_select(out=ident[:, :], in_=ident[:, :], compare_op=ALU.not_equal, fill=1.0,
                            base=0, pattern=[[-1, P]], channel_multiplier=1).then_inc(s_const, 1)
            g.memset(ones[:, :], 1.0 / C).then_inc(s_const, 1)
            g.memset(mhalf[:, :], -0.5).then_inc(s_const, 1)
            g.wait_ge(s_const, 3)
            g.wait_ge(s_cond, 1)
            for n in range(1, ND, 2):
                j, ct = DIAG_LAGS[n // CT], n % CT
                g.tensor_scalar(diag[:, n, :], ident[:, :], condT[:, ct, T - 1 - j:T - j], 0.0,
                                ALU.mult, ALU.add).then_inc(s_diag[1], 1)

            def low_parts(hg, pieces):
                for p in pieces:
                    cols = slice(PIECE * p, PIECE * (p + 1))
                    g.wait_ge(s_whi, hg * 8 + (p + 1))
                    g.tensor_tensor(wl[:, cols], raw[:, cols], wh[:, cols].bitcast(F32), ALU.subtract)\
                        .then_inc(s_wlo, 1)

            def rstd(n):
                nt = NORMS[n][1] // P
                g.wait_ge(s_ve, n + 1)
                g.tensor_tensor(rs[:, 0:nt], ve[:, 0:nt], mhalf[:, 0:nt], ALU.pow).then_inc(s_rs, 1)

            low_parts(0, range(0, 2))
            rstd(0)
            low_parts(0, range(2, 6))
            g.memset(pt[:, :, :, :, :], 0.0).then_inc(s_zero, 1)
            rstd(1)
            low_parts(0, range(6, 8))
            rstd(2)
            low_parts(1, range(0, 6))
            with g.Fori(1, NG - 1) as hg:
                low_parts(hg, range(6, 8))
                low_parts(hg + 1, range(0, 6))
            low_parts(NG - 1, range(6, 8))
            low_parts(NG, range(0, 4))
            rstd(3)
            low_parts(NG, range(4, 8))

            def hidden_low(n, m):
                g.wait_ge(s_hhi, MT * n + m + 1)
                g.tensor_tensor(hl[:, m, :], hf[:, m % 4, :], hh[:, m, :].bitcast(F32), ALU.subtract)\
                    .then_inc(s_hlo[0], 1)

            for m in (0, 2, 4):
                hidden_low(0, m)
            rstd(4)
            hidden_low(0, 6)
            for m in (0, 2, 4, 6):
                hidden_low(1, m)

        @block.scalar
        def _(a):
            a.dma_start(crow[:, :], cond).then_inc(s_row[0], 16)

            def high_parts(hg, pieces):
                first = isinstance(hg, int) and hg == 0
                for p in pieces:
                    cols = slice(PIECE * p, PIECE * (p + 1))
                    if p % 2 == 0:
                        a.wait_ge(s_raw[p // 2], hg * 16 + 16)
                        if not first:
                            if p < 6:
                                a.wait_ge(s_proj, hg * 24 - 8 + 4 * (p // 2))
                            else:
                                a.wait_ge(s_y, hg * 4)
                    a.activation(wh[:, cols], raw[:, cols], ACT.Copy).then_inc(s_whi, 1)

            a.wait_ge(s_const, 3)
            a.activation(rs[:, :], mhalf[:, :], ACT.Copy)
            a.wait_ge(s_cond, 1)
            for n in range(0, ND, 2):
                j, ct = DIAG_LAGS[n // CT], n % CT
                a.activation(diag[:, n, :], ident[:, :], ACT.Copy,
                             scale=condT[:, ct, T - 1 - j:T - j]).then_inc(s_diag[0], 1)
                if n == 6:
                    a.wait_ge(s_xt, 2)
                    for c in range(CT):
                        a.activation(part(x0, c, CHUNKS[1]), OB[1][:, 256 * c:256 * (c + 1)], ACT.Copy)\
                            .then_inc(s_xe[1], 1)
            for ct in range(CT):
                a.wait_ge(s_xt, 3 + ct)
                a.activation(part(x0, ct, CHUNKS[2]), YB[ct][:, :], ACT.Copy).then_inc(s_xe[2], 1)

            def group_biases(hg, first, count):
                if not (isinstance(hg, int) and hg == 0):
                    if first == 0:
                        a.wait_ge(s_ev, hg * 24)
                    else:
                        a.wait_ge(s_ohi, hg * 8)
                    a.sem_inc(s_bgfree, 1)
                if isinstance(hg, int) and hg == 0:
                    a.wait_ge(s_btc, 1)
                src = bT[:, B_QKV:B_QKV + 3 * NH].rearrange("p (w g h) -> p w g h", w=3, g=NG)
                a.activation(bg[:, first:first + count, :], src[:, first:first + count, bass.ds(hg, 1), :]
                             .rearrange("p w g h -> p w (g h)"), ACT.Copy).then_inc(s_bg, 1)

            def squares(n):
                for ct in range(CT):
                    a.wait_ge(s_xm, CT * n + ct + 1)
                    a.activation(ln_sq(n, ct), ln_c(n, ct), ACT.Square).then_inc(s_sq, 1)

            def x1_high(n):
                for ct in range(CT):
                    a.wait_ge(s_x1f, CT * n + ct + 1)
                    a.activation(part(x1h, ct, NORMS[n]), ln_c(n, ct), ACT.Copy).then_inc(s_hi, 1)

            a.wait_ge(s_bt, 1)
            a.activation(bT[:, :], PB[2][:, 0:NBIAS], ACT.Copy).then_inc(s_btc, 1)
            high_parts(0, range(0, 2))
            squares(0)
            high_parts(0, range(2, 4))
            group_biases(0, 0, 3)
            high_parts(0, range(4, 5))
            x1_high(0)
            high_parts(0, range(5, 6))

            def evac(hg, u, j):
                a.wait_ge(s_proj, hg * 24 + (12 * u + j + 1))
                src = PB[j % 3][:, :]
                if j < 2 * GH:
                    dst = (q_sb if j < GH else k_sb)[:, j % GH, :]
                    a.activation(dst, src, ACT.Identity, bias=bg[:, j // GH, j % GH:j % GH + 1])\
                        .then_inc(s_ev, 1)
                else:
                    a.activation(v_sb[:, u, j - 2 * GH, :], src, ACT.Copy).then_inc(s_ev, 1)

            def evac_chunk(j):
                chunk, i = divmod(j, 6)
                t0, nt = CHUNKS[chunk]
                a.wait_ge(s_proj, j + 1)
                if i < 4:
                    for h in range(2):
                        head = 2 * (i % 2) + h
                        m = a.activation((q_sb if i < 2 else k_sb)[:, head, t0:t0 + nt],
                                         PB[j % 3][:, nt * h:nt * (h + 1)], ACT.Identity,
                                         bias=bg[:, i // 2, head:head + 1])
                    m.then_inc(s_ev, 1)
                else:
                    a.activation(v_sb[:, 0, t0 // P + i - 4, :], PB[j % 3][:, :], ACT.Copy).then_inc(s_ev, 1)

            def exps(hg, u):
                a.wait_ge(s_sd, hg * 2 + (u + 1))
                a.activation(pe_[:, :], sd[:, :], ACT.Exp, scale=SCALE).then_inc(s_e, 1)

            def o_high(hg, prev, heads):
                for h in heads:
                    a.wait_ge(s_pv, hg * 8 + (4 * prev + h + 1))
                    a.activation(oh[:, h, :], OB[h % 2][:, :], ACT.Identity,
                                 bias=bg[:, 2, h:h + 1]).then_inc(s_ohi, 1)

            def second_half(hg, last=False):
                for j in (5, 6, 7, 8):
                    evac(hg, 1, j)
                    if j == 5:
                        high_parts(hg + 1, range(0, 2))
                high_parts(hg + 1, range(2, 4))
                exps(hg, 1)
                evac(hg, 1, 9)
                if last:
                    squares(3)
                evac(hg, 1, 10)
                evac(hg, 1, 11)
                high_parts(hg + 1, range(4, 6))

            def group(hg, last=False):
                group_biases(hg, 0, 2)
                a.wait_ge(s_bg, hg * 2)
                for j in range(4):
                    evac(hg, 0, j)
                o_high(hg, -1, (0, 1))
                evac(hg, 0, 4)
                o_high(hg, -1, (2, 3))
                group_biases(hg, 2, 1)
                for j in (5, 6, 7, 8, 9):
                    evac(hg, 0, j)
                    if j == 7:
                        high_parts(hg, range(6, 8))
                exps(hg, 0)
                evac(hg, 0, 10)
                evac(hg, 0, 11)
                a.wait_ge(s_bg, hg * 2 + 1)
                for j in range(4):
                    evac(hg, 1, j)
                o_high(hg, 0, (0, 1))
                evac(hg, 1, 4)
                o_high(hg, 0, (2, 3))
                second_half(hg, last)

            a.wait_ge(s_bg, 1)
            for j in range(UNIT_BANKS):
                if j == UNIT_BANKS - 1:
                    exps(0, 0)
                evac_chunk(j)
                if j == 0:
                    squares(1)
                if j == 4:
                    x1_high(1)
            high_parts(0, range(6, 8))
            squares(2)
            o_high(0, 0, range(GH))
            x1_high(2)
            for j in range(5):
                evac(0, 1, j)
            second_half(0)
            with a.Fori(1, NG - 1) as hg:
                group(hg)
            group(NG - 1, last=True)
            o_high(NG, -1, range(GH))
            x1_high(3)
            high_parts(NG, range(6, 8))

            def hidden(n, m):
                a.wait_ge(s_f1, MT * n + m + 1)
                if MT * n + m >= 4:
                    a.wait_ge(s_hlo[m % 2], (MT * n + m - 4) // 2 + 1)
                a.activation(hf[:, m % 4, :], PB[m % 3][:, :], ACT.Gelu,
                             bias=bT[:, B_F1 + m:B_F1 + m + 1]).then_inc(s_hf, 1)
                a.wait_ge(s_hf, MT * n + m + 1)
                a.activation(hh[:, m, :], hf[:, m % 4, :], ACT.Copy).then_inc(s_hhi, 1)

            for m in range(MT):
                hidden(0, m)
                if m == 3:
                    squares(4)
            x1_high(4)
            for m in range(MT):
                hidden(1, m)
            for n in range(HALVES):
                a.wait_ge(s_ft, 2 * n + 2)
                a.activation(otok[:, 0, 2 * n + 1, :], OB[1][:, :], ACT.Copy).then_inc(s_fe[1], 1)

        @block.vector
        def _(v):
            v.wait_ge(s_condt, 1)
            v.tensor_copy(condT[:, :, :], S_BANK[:, 0:CT * B].rearrange("p (k b) -> p k b", k=CT))\
                .then_inc(s_cond, 1)
            v.wait_ge(s_xt, 1)
            for ct in range(CT):
                v.tensor_copy(part(x0, ct, CHUNKS[0]), OB[0][:, 256 * ct:256 * (ct + 1)]).then_inc(s_xe[0], 1)

            def conv(n, i0, i1):
                for i in range(i0, i1):
                    j = DVE_LAGS[n][i]
                    for ct in range(CT):
                        xs = by_batch(part(x0, ct, CHUNKS[n]))
                        acc = by_batch(part(xc, ct, CHUNKS[n]))
                        w = condT[:, ct, T - 1 - j:T - j]
                        if i == 0:
                            v.scalar_tensor_tensor(out=acc[:, :, j:], in0=xs[:, :, :T - j], scalar=w,
                                                   in1=xs[:, :, j:], op0=ALU.mult, op1=ALU.add).then_inc(s_cdve, 1)
                            v.tensor_copy(acc[:, :, 0:j], xs[:, :, 0:j]).then_inc(s_cdve, 1)
                        else:
                            v.wait_ge(s_cdve, DVE_STEPS[n] + (2 * (ct + 1) if i == 1 else CT * i + ct + 1))
                            v.scalar_tensor_tensor(out=acc[:, :, j:], in0=xs[:, :, :T - j], scalar=w,
                                                   in1=acc[:, :, j:], op0=ALU.mult, op1=ALU.add).then_inc(s_cdve, 1)

            def conv_sum(n):
                nt = CHUNKS[n][1]
                v.wait_ge(s_cdve, DVE_STEPS[n + 1])
                for ct in range(CT):
                    v.wait_ge(s_cpe, CT * n + ct + 1)
                    acc = part(xc, ct, CHUNKS[n])
                    v.tensor_tensor(acc, acc, CONV_BANKS[n][ct][:, 0:nt], ALU.add).then_inc(s_in, 1)

            def centre(n):
                v.wait_ge(s_mean, n + 1)
                v.wait_ge(s_in, CT * (n + 1))
                for ct in range(CT):
                    v.tensor_tensor(ln_c(n, ct), ln_in(n, ct), STAT_BANK[n][:, 0:NORMS[n][1]], ALU.subtract)\
                        .then_inc(s_xm, 1)

            def scale_up(n):
                for ct in range(CT):
                    v.wait_ge(s_sq, CT * n + ct + 1)
                    c = by_batch(ln_c(n, ct))
                    v.tensor_tensor(c, c, ada(SCALE1 if n < NC else SCALE2, ct, NORMS[n]), ALU.mult)\
                        .then_inc(s_sc, 1)

            def var_eps(n):
                v.wait_ge(s_var, n + 1)
                if n < 2:
                    nt = NORMS[n][1] // P
                    v.tensor_scalar(ve[:, 0:nt], STAT_BANK[n][:, 0:nt], EPS, None, ALU.add).then_inc(s_ve, 1)
                else:
                    v.transpose(vt[:, :, :], STAT_BANK[n][:, 0:P].rearrange("p (k r) -> p k r", r=T))\
                        .then_inc(s_vt, 1)
                    v.wait_ge(s_vt, n - 1)
                    v.tensor_scalar(ve[:, :], vt[:, :, 0:1].rearrange("p k r -> p (k r)"), EPS, None, ALU.add)\
                        .then_inc(s_ve, 1)

            def norm(n):
                v.wait_ge(s_rb, n + 1)
                v.wait_ge(s_sc, CT * (n + 1))
                for ct in range(CT):
                    v.tensor_tensor(ln_c(n, ct), ln_c(n, ct), RSTD_BANK[n][:, 0:NORMS[n][1]], ALU.mult)\
                        .then_inc(s_mod, 1)

            def shift(n):
                for ct in range(CT):
                    v.wait_ge(s_mod, CT * n + ct + 1)
                    c = by_batch(ln_c(n, ct))
                    v.tensor_tensor(c, c, ada(SHIFT1 if n < NC else SHIFT2, ct, NORMS[n]), ALU.add)\
                        .then_inc(s_x1f, 1)

            def x1_low(n):
                for ct in range(CT):
                    v.wait_ge(s_hi, CT * n + ct + 1)
                    v.tensor_tensor(part(x1l, ct, NORMS[n]), ln_c(n, ct),
                                    part(x1h, ct, NORMS[n]).bitcast(F32), ALU.subtract).then_inc(s_lo, 1)

            def modulation(i):
                (m0, m1), n = ADA_PARTS[i], ADA_PARTS[i][1] - ADA_PARTS[i][0]
                v.wait_ge(s_adap, i + 1)
                v.tensor_tensor(adaT[:, m0:m1, :], ADA_BANKS[i][:, 0:n * B].rearrange("p (m b) -> p m b", b=B),
                                bT[:, B_ADA + m0:B_ADA + m1].unsqueeze(2).to_broadcast([P, n, B]),
                                ALU.add).then_inc(s_adat, 1)

            def one_plus(i, scale):
                v.wait_ge(s_adat, ADA_STEPS[i])
                sc = adaT[:, CT * scale:CT * (scale + 1), :]
                v.tensor_scalar(sc, sc, 1.0, None, ALU.add).then_inc(s_adat, 1)
                v.wait_ge(s_adat, ADA_STEPS[i] + 1)

            def softmax_front(hg, u):
                scores = S_BANK[:, :].rearrange("p (n k) -> p n k", k=T)
                v.wait_ge(s_s, hg * 2 + (u + 1))
                v.tensor_reduce(mx[:, :], scores, AX_X, ALU.max).then_inc(s_mx, 1)
                v.wait_ge(s_mx, hg * 2 + (u + 1))
                v.tensor_tensor(sd[:, :].rearrange("p (n k) -> p n k", k=T), scores,
                                mx[:, :].unsqueeze(2).to_broadcast([P, GH * TG, T]), ALU.subtract)\
                    .then_inc(s_sd, 1)

            def softmax_probs(hg, u):
                e3 = pe_[:, :].rearrange("p (n k) -> p n k", k=T)
                v.wait_ge(s_e, hg * 2 + (u + 1))
                v.tensor_reduce(sm[:, :], e3, AX_X, ALU.add).then_inc(s_sum, 1)
                v.wait_ge(s_sum, hg * 2 + (u + 1))
                v.reciprocal(rc[:, :], sm[:, :]).then_inc(s_rc, 1)
                v.wait_ge(s_rc, hg * 2 + (u + 1))
                v.tensor_tensor(pn[:, :].rearrange("p (n k) -> p n k", k=T), e3,
                                rc[:, :].unsqueeze(2).to_broadcast([P, GH * TG, T]), ALU.mult)\
                    .then_inc(s_pn, 1)

            def softmax_transpose(hg, u, heads=slice(0, GH)):
                v.wait_ge(s_pn, hg * 2 + (u + 1))
                cols = slice(heads.start * TG * T, heads.stop * TG * T)
                for b in range(QB):
                    rows_b = slice(T * b, T * (b + 1))
                    dst = pt[rows_b, u, heads, :, T * b:T * (b + 1)].rearrange("p h g q -> p (h g) q")
                    v.transpose(dst, pn[rows_b, cols].rearrange("p (n k) -> p n k", k=T)).then_inc(s_pt, 1)

            def softmax_back(hg, u):
                softmax_probs(hg, u)
                softmax_transpose(hg, u)

            def o_low(hg, prev, heads):
                group = hg if prev >= 0 else hg - 1
                for h in heads:
                    v.wait_ge(s_ohi, hg * 8 + (4 * prev + h + 1))
                    v.scalar_tensor_tensor(out=ol[:, h, :], in0=OB[h % 2][:, :],
                                           scalar=bT[:, bass.ds(group * GH + (2 * NH + h), 1)],
                                           in1=oh[:, h, :].bitcast(F32), op0=ALU.add, op1=ALU.subtract)\
                        .then_inc(s_olo, 1)

            def add_y(hg, prev, first=False):
                hn = prev % 2
                for ct in range(CT):
                    v.wait_ge(s_y, hg * 4 + (2 * prev + ct + 1))
                    if first:
                        v.tensor_copy(half(yacc, ct, hn), YB[ct][:, :]).then_inc(s_ya, 1)
                    else:
                        v.wait_ge(s_ya, hg * 4 + (2 * prev + ct - 3))
                        v.tensor_tensor(half(yacc, ct, hn), half(yacc, ct, hn), YB[ct][:, :], ALU.add)\
                            .then_inc(s_ya, 1)

            def unit(hg, u, first_y=False):
                o_low(hg, u - 1, range(GH))
                add_y(hg, u - 1, first_y)
                softmax_front(hg, u)
                softmax_back(hg, u)

            v.wait_ge(s_cond, 1)
            v.wait_ge(s_xe[0], CT)
            conv(0, 0, len(DVE_LAGS[0]))
            conv_sum(0)
            centre(0)
            v.wait_ge(s_btc, 1)
            modulation(0)
            one_plus(0, SCALE1)
            v.wait_ge(s_xe[1], CT)
            conv(1, 0, 1)
            var_eps(0)
            scale_up(0)
            conv(1, 1, 3)
            norm(0)
            shift(0)
            conv(1, 3, 5)
            x1_low(0)
            conv(1, 5, len(DVE_LAGS[1]))
            conv_sum(1)
            v.wait_ge(s_xe[2], CT)
            conv(2, 0, 1)
            centre(1)
            conv(2, 1, 2)
            scale_up(1)
            var_eps(1)
            conv(2, 2, 4)
            norm(1)
            shift(1)
            conv(2, 4, 5)
            x1_low(1)
            conv(2, 5, len(DVE_LAGS[2]))
            softmax_front(0, 0)
            softmax_probs(0, 0)
            v.wait_ge(s_zero, 1)
            softmax_transpose(0, 0)
            conv_sum(2)
            centre(2)
            o_low(0, 0, (0, 1))
            scale_up(2)
            var_eps(2)
            o_low(0, 0, (2,))
            norm(2)
            shift(2)
            o_low(0, 0, (3,))
            x1_low(2)
            modulation(1)
            modulation(2)
            add_y(0, 0, first=True)
            one_plus(2, SCALE2)
            softmax_front(0, 1)
            softmax_back(0, 1)
            unit(1, 0, first_y=True)
            unit(1, 1)
            with v.Fori(2, NG - 1) as hg:
                unit(hg, 0)
                unit(hg, 1)
            unit(NG - 1, 0)

            def residual(n):
                span = NORMS[NC + n]
                for ct in range(CT):
                    v.wait_ge(s_ya, 2 * (2 * (NG - 1) + n) + ct + 1)
                    y = by_batch(half(yacc, ct, n))
                    v.scalar_tensor_tensor(out=y, in0=y, scalar=bT[:, B_OUT + ct:B_OUT + ct + 1],
                                           in1=ada(GATE1, ct, span), op0=ALU.add, op1=ALU.mult).then_inc(s_res, 1)
                for ct in range(CT):
                    v.wait_ge(s_res, CT * n + ct + 1)
                    v.tensor_tensor(half(yacc, ct, n), half(yacc, ct, n), half(xc, ct, n), ALU.add)\
                        .then_inc(s_in, 1)

            def residual_sum(n):
                for ct in range(CT):
                    v.wait_ge(s_in, CT * (NC + n) + ct + 1)
                    v.tensor_tensor(half(xc, ct, n), half(xc, ct, n), half(yacc, ct, n), ALU.add)\
                        .then_inc(s_xs, 1)

            o_low(NG - 1, 0, range(GH))
            add_y(NG - 1, 0)
            residual(0)
            softmax_front(NG - 1, 1)
            centre(3)
            softmax_probs(NG - 1, 1)
            softmax_transpose(NG - 1, 1, slice(0, 2))
            var_eps(3)
            softmax_transpose(NG - 1, 1, slice(2, GH))
            o_low(NG, -1, (0,))
            scale_up(3)
            o_low(NG, -1, (1,))
            norm(3)
            o_low(NG, -1, (2,))
            shift(3)
            o_low(NG, -1, (3,))
            x1_low(3)
            add_y(NG, -1)
            residual(1)

            def hidden_low(n, m):
                v.wait_ge(s_hhi, MT * n + m + 1)
                v.tensor_tensor(hl[:, m, :], hf[:, m % 4, :], hh[:, m, :].bitcast(F32), ALU.subtract)\
                    .then_inc(s_hlo[1], 1)

            hidden_low(0, 1)
            centre(4)
            hidden_low(0, 3)
            scale_up(4)
            var_eps(4)
            residual_sum(0)
            hidden_low(0, 5)
            norm(4)
            shift(4)
            hidden_low(0, 7)
            x1_low(4)
            residual_sum(1)

            def gated(piece):
                n, ct, bank, toks = FFN2_PIECES[piece]
                span = (n * HT + toks.start, toks.stop - toks.start)
                dst = part(x0, ct, span)
                v.wait_ge(s_f2, piece + 1)
                v.scalar_tensor_tensor(out=by_batch(dst), in0=by_batch(bank),
                                       scalar=bT[:, B_F2 + ct:B_F2 + ct + 1],
                                       in1=ada(GATE2, ct, span), op0=ALU.add, op1=ALU.mult)\
                    .then_inc(s_gt, 1)
                v.wait_ge(s_gt, piece + 1)
                v.wait_ge(s_xs, CT * n + ct + 1)
                v.tensor_tensor(dst, dst, part(xc, ct, span), ALU.add).then_inc(s_fin, 1)

            def store_copy(n):
                v.wait_ge(s_ft, 2 * n + 1)
                v.tensor_copy(otok[:, 0, 2 * n, :], S_BANK[:, :]).then_inc(s_fe[0], 1)

            gated(0)
            gated(1)
            for m in (1, 3, 5, 7):
                hidden_low(1, m)
            store_copy(0)
            gated(2)
            gated(3)
            gated(4)
            store_copy(1)

        @block.tensor
        def _(pe):
            pe.wait_ge(s_const, 1)
            pe.wait_ge(s_row[0], 16)
            for ct in range(CT):
                m = pe.transpose(S_BANK[:, B * ct:B * (ct + 1)], crow[:, ct * P:(ct + 1) * P], ident[0:B, 0:B])
            m.then_inc(s_condt, 1)
            for n in range(2):
                t0, nt = CHUNKS[n][0] // P, CHUNKS[n][1] // P
                pe.wait_ge(s_x[n], 16)
                for ct in range(CT):
                    for t in range(nt):
                        c0 = ct * nt * P + t * P
                        m = pe.transpose(OB[n][:, c0:c0 + P], xtok[:, t0 + t, ct * P:(ct + 1) * P], ident[:, :])
                m.then_inc(s_xt, 1)

            def conv(n, i0, i1):
                nt, last = CHUNKS[n][1], len(PE_LAGS[n]) - 1
                for i in range(i0, i1):
                    j = PE_LAGS[n][i]
                    for ct in range(CT):
                        d = DIAG_LAGS.index(j)
                        pe.wait_ge(s_diag[ct], d + 1)
                        xs = by_batch(part(x0, ct, CHUNKS[n]))
                        dst = by_batch(CONV_BANKS[n][ct][:, 0:nt])
                        m = pe.matmul(dst[:, :, j:], diag[:, CT * d + ct, :], xs[:, :, :T - j],
                                      start=(i == 0), stop=(i == last))
                        if i == last:
                            m.then_inc(s_cpe, 1)

            def mean(n):
                pe.wait_ge(s_const, 2)
                pe.wait_ge(s_in, CT * (n + 1))
                for ct in range(CT):
                    m = pe.matmul(STAT_BANK[n][:, 0:NORMS[n][1]], ones[:, :], ln_in(n, ct),
                                  start=(ct == 0), stop=(ct == CT - 1))
                m.then_inc(s_mean, 1)

            def var(n):
                pe.wait_ge(s_sq, CT * (n + 1))
                if n < 2:
                    for t in range(NORMS[n][1] // P):
                        for ct in range(CT):
                            m = pe.matmul(STAT_BANK[n][:, t:t + 1], ln_sq(n, ct)[:, t * P:(t + 1) * P],
                                          ones[:, 0:1], start=(ct == 0), stop=(ct == CT - 1))
                else:
                    for ct in range(CT):
                        for t in range(TG):
                            m = pe.matmul(STAT_BANK[n][T * t:T * (t + 1), 0:P], ones[:, 0:T],
                                          ln_sq(n, ct)[:, t * P:(t + 1) * P], start=(ct == 0), stop=(ct == CT - 1))
                m.then_inc(s_var, 1)

            def spread(n):
                pe.wait_ge(s_rs, n + 1)
                for k in range(NORMS[n][1] // P):
                    if n < 2:
                        dst = RSTD_BANK[n][:, k * P:(k + 1) * P]
                    else:
                        dst = RSTD_BANK[n][:, :].rearrange("p (t k r) -> p k t r", t=TG, r=T)[:, k]
                    m = pe.matmul(dst, rs[:, k:k + 1].to_broadcast([P, P]), ident[:, :], start=True, stop=True)
                m.then_inc(s_rb, 1)

            def modulation(i):
                m0, m1 = ADA_PARTS[i]
                for c in range(m0, m1):
                    for kt in range(CT):
                        m = pe.matmul(ADA_BANKS[i][:, (c - m0) * B:(c - m0 + 1) * B],
                                      adaw[:, kt, c * P:(c + 1) * P], condT[:, kt, :],
                                      start=(kt == 0), stop=(kt == CT - 1))
                m.then_inc(s_adap, 1)

            pe.wait_ge(s_xe[0], CT)
            conv(0, 0, 4)
            pe.wait_ge(s_x[2], 16)
            for ct in range(CT):
                for t in range(TG):
                    m = pe.transpose(YB[ct][:, t * P:(t + 1) * P], xtok[:, TG + t, ct * P:(ct + 1) * P], ident[:, :])
                m.then_inc(s_xt, 1)
            conv(0, 4, 8)
            pe.wait_ge(s_row[1], 16 * 5)
            pe.transpose(PB[2][:, 0:NBIAS], rows[:, :], ident[0:NBIAS, 0:NBIAS]).then_inc(s_bt, 1)
            conv(0, 8, len(PE_LAGS[0]))
            pe.wait_ge(s_adaw[0], 16)
            pe.wait_ge(s_btc, 1)
            modulation(0)
            mean(0)
            pe.wait_ge(s_xe[1], CT)
            pe.wait_ge(s_xe[2], CT)
            conv(1, 0, 2)
            var(0)
            conv(1, 2, 4)
            spread(0)
            conv(1, 4, len(PE_LAGS[1]))

            def three(dst, w_cols, act, start, stop):
                a_hi, a_lo = act
                pe.matmul(dst, wl[:, w_cols], a_hi, start=start, stop=False)
                pe.matmul(dst, wh[:, w_cols], a_lo, start=False, stop=False)
                return pe.matmul(dst, wh[:, w_cols], a_hi, start=False, stop=stop)

            def v_tile(dst, t0):
                tk = slice(t0, t0 + P)
                for kt in range(CT):
                    wc = slice(2048 + PIECE * kt, 2048 + PIECE * (kt + 1))
                    pe.matmul(dst, x1l[:, kt, tk], wh[:, wc], start=(kt == 0), stop=False)
                    pe.matmul(dst, x1h[:, kt, tk], wl[:, wc], start=False, stop=False)
                    m = pe.matmul(dst, x1h[:, kt, tk], wh[:, wc], start=False, stop=(kt == CT - 1))
                return m

            def project(hg, u, js):
                toks = slice(u * HT, (u + 1) * HT)
                for j in js:
                    if j % GH == 0:
                        pe.wait_ge(s_wlo, hg * 8 + (2 * (j // GH) + 2))
                    pe.wait_ge(s_ev, hg * 24 + (12 * u + j - 2))
                    dst = PB[j % 3][:, :]
                    if j < 2 * GH:
                        for kt in range(CT):
                            c0 = 1024 * (j // GH) + PIECE * kt + P * (j % GH)
                            m = three(dst, slice(c0, c0 + P), (x1h[:, kt, toks], x1l[:, kt, toks]),
                                      kt == 0, kt == CT - 1)
                    else:
                        m = v_tile(dst, u * HT + P * (j - 2 * GH))
                    m.then_inc(s_proj, 1)

            def project_chunk(chunk, banks_of):
                t0, nt = CHUNKS[chunk]
                toks = slice(t0, t0 + nt)
                for i in banks_of:
                    j = 6 * chunk + i
                    if i % 2 == 0:
                        pe.wait_ge(s_wlo, i + 2)
                    if j >= 3:
                        pe.wait_ge(s_ev, j - 2)
                    if i < 4:
                        for h in range(2):
                            for kt in range(CT):
                                c0 = 1024 * (i // 2) + PIECE * kt + P * (2 * (i % 2) + h)
                                m = three(PB[j % 3][:, nt * h:nt * (h + 1)], slice(c0, c0 + P),
                                          (x1h[:, kt, toks], x1l[:, kt, toks]), kt == 0, kt == CT - 1)
                    else:
                        m = v_tile(PB[j % 3][:, :], t0 + P * (i - 4))
                    m.then_inc(s_proj, 1)

            def scores(hg, u):
                pe.wait_ge(s_ev, hg * 24 + (12 * u + (2 * GH if not (isinstance(hg, int) and hg + u == 0) else 10)))
                if not (isinstance(hg, int) and hg + u == 0):
                    pe.wait_ge(s_sd, hg * 2 + u)
                for h in range(GH):
                    for t in range(TG):
                        for b in range(QB):
                            c = t * P + b * T
                            m = pe.matmul(S_BANK[b * T:(b + 1) * T, (h * TG + t) * T:(h * TG + t + 1) * T],
                                          q_sb[:, h, c:c + T], k_sb[:, h, c:c + T], start=True, stop=True)
                m.then_inc(s_s, 1)

            def attend(hg, prev, h, first=False):
                hn = prev % 2
                if h == 0:
                    pe.wait_ge(s_pt, hg * 8 + (4 * prev + 4))
                    pe.wait_ge(s_ev, hg * 24 + (12 * prev + 12))
                if not (first and h < 2):
                    pe.wait_ge(s_olo, hg * 8 + (4 * prev + h - 1))
                for t in range(TG):
                    m = pe.matmul(OB[h % 2][:, t * P:(t + 1) * P], v_sb[:, hn, t, h * P:(h + 1) * P],
                                  pt[:, hn, h, t, :], start=True, stop=True)
                m.then_inc(s_pv, 1)

            def out_proj(hg, prev, h, first=False):
                pe.wait_ge(s_olo, hg * 8 + (4 * prev + h + 1))
                if h == 0:
                    pe.wait_ge(s_wlo, (hg if prev >= 0 else hg - 1) * 8 + 8)
                    if not first:
                        pe.wait_ge(s_ya, hg * 4 + 2 * prev)
                for ct in range(CT):
                    c0 = 3072 + C * h + P * ct
                    m = three(YB[ct][:, :], slice(c0, c0 + P), (oh[:, h, :], ol[:, h, :]), h == 0, h == GH - 1)
                    if h == GH - 1:
                        m.then_inc(s_y, 1)

            def unit(hg, u, last=False):
                project(hg, u, range(0, 4))
                attend(hg, u - 1, 0)
                attend(hg, u - 1, 1)
                project(hg, u, (4,))
                attend(hg, u - 1, 2)
                out_proj(hg, u - 1, 0)
                attend(hg, u - 1, 3)
                for h in (1, 2, 3):
                    out_proj(hg, u - 1, h)
                project(hg, u, (5, 6, 7, 8))
                scores(hg, u)
                if last:
                    mean(3)
                project(hg, u, (9, 10, 11))
                if last:
                    var(3)

            pe.wait_ge(s_lo, CT)
            pe.wait_ge(s_adat, 2)
            project_chunk(0, (0,))
            mean(1)
            project_chunk(0, (1, 2))
            var(1)
            project_chunk(0, (3,))
            spread(1)
            project_chunk(0, (4, 5))
            conv(2, 0, 4)
            pe.wait_ge(s_lo, CT * 2)
            project_chunk(1, range(0, 5))
            scores(0, 0)
            project_chunk(1, (5,))
            conv(2, 4, len(PE_LAGS[2]))
            pe.wait_ge(s_adaw[1], 16)
            pe.wait_ge(s_ev, UNIT_BANKS)
            modulation(1)
            pe.wait_ge(s_sd, 1)
            mean(2)
            attend(0, 0, 0, True)
            attend(0, 0, 1, True)
            var(2)
            modulation(2)
            attend(0, 0, 2, True)
            out_proj(0, 0, 0, True)
            spread(2)
            attend(0, 0, 3, True)
            for h in (1, 2, 3):
                out_proj(0, 0, h, True)
            pe.wait_ge(s_lo, CT * 3)
            pe.wait_ge(s_adat, ADA_STEPS[2])
            project(0, 1, range(0, 9))
            scores(0, 1)
            project(0, 1, (9, 10, 11))
            with pe.Fori(1, NG - 1) as hg:
                unit(hg, 0)
                unit(hg, 1)
            unit(NG - 1, 0)
            unit(NG - 1, 1, last=True)
            attend(NG, -1, 0)
            attend(NG, -1, 1)
            pe.wait_ge(s_sd, 2 * NG)
            spread(3)
            pe.wait_ge(s_pt, 8 * NG + 4)
            attend(NG, -1, 2)
            out_proj(NG, -1, 0)
            attend(NG, -1, 3)
            for h in (1, 2, 3):
                out_proj(NG, -1, h)

            def ffn1(n, tiles):
                if 0 in tiles:
                    pe.wait_ge(s_lo, CT * (NC + n + 1))
                    pe.wait_ge(s_wlo, 8 * NG + 4)
                toks = slice(n * HT, (n + 1) * HT)
                for i in tiles:
                    if i >= 3 or n:
                        pe.wait_ge(s_hf, MT * n + max(i - 2, 0))
                    for kt in range(CT):
                        c0 = MLP * kt + P * i
                        m = three(PB[i % 3][:, :], slice(c0, c0 + P), (x1h[:, kt, toks], x1l[:, kt, toks]),
                                  kt == 0, kt == CT - 1)
                    m.then_inc(s_f1, 1)

            def ffn2(piece, k):
                n, ct, bank, toks = FFN2_PIECES[piece]
                pe.wait_ge(s_hlo[k % 2], (MT * n + k) // 2 + 1)
                c0 = 2048 + C * k + P * ct
                m = three(bank, slice(c0, c0 + P), (hh[:, k, toks], hl[:, k, toks]), k == 0, k == MT - 1)
                if k == MT - 1:
                    m.then_inc(s_f2, 1)

            def result_transposes(n, pair):
                pe.wait_ge(s_fin, CT * (n + 1) + n * pair)
                bank = (S_BANK, OB[1])[pair]
                if n:
                    pe.wait_ge(s_fe[pair], n)
                for i in range(2):
                    for ct in range(CT):
                        t = 2 * pair + i
                        m = pe.transpose(bank[:, C * i + P * ct:C * i + P * (ct + 1)],
                                         half(x0, ct, n)[:, t * P:(t + 1) * P], ident[:, :])
                m.then_inc(s_ft, 1)

            ffn1(0, range(0, 4))
            mean(4)
            ffn1(0, range(4, 6))
            var(4)
            ffn1(0, range(6, 8))
            spread(4)
            pe.wait_ge(s_wlo, 8 * NG + 8)
            pe.wait_ge(s_ya, 4 * NG)
            for k in range(MT):
                ffn2(0, k)
                ffn2(1, k)
            ffn1(1, range(MT))
            result_transposes(0, 0)
            result_transposes(0, 1)
            for piece in (2, 3):
                for k in range(MT):
                    ffn2(piece, k)
            for k in range(MT):
                ffn2(4, k)
                if k == MT - 3:
                    result_transposes(1, 0)
            result_transposes(1, 1)


_INS = ['x', 'cond_2048', 'L1_cond_ada_w', 'L1_cond_ada_b', 'L1_cond_qkv_w', 'L1_cond_qkv_b', 'L1_cond_out_w',
        'L1_cond_out_b', 'L1_cond_ffn_w1', 'L1_cond_ffn_b1', 'L1_cond_ffn_w2', 'L1_cond_ffn_b2']
_OUTS = [((32, 32, 256), 'float32')]


def kernel(**inputs):
    import numpy as _np
    import concourse.bacc as _bacc
    from concourse import mybir as _mybir
    from concourse.bass_utils import run_bass_kernel_spmd as _run

    nc = _bacc.Bacc("TRN2", target_bir_lowering=False, num_devices=1)
    arrays, args = {}, []
    for name in _INS:
        a = _np.ascontiguousarray(inputs[name])
        arrays[f"in_{name}_dram"] = a
        args.append(nc.dram_tensor(f"in_{name}_dram", a.shape, _mybir.dt.from_np(a.dtype), kind="ExternalInput").ap())
    for i, (shape, dtype) in enumerate(_OUTS):
        dt = _mybir.dt.from_np(_np.dtype(dtype))
        args.append(nc.dram_tensor(f"out_{i}_dram", shape, dt, kind="ExternalOutput").ap())
    cond_resid_block_kernel(nc, *args)
    r = _run(nc, [arrays], core_ids=[0])
    got = tuple(r.results[0][f"out_{i}_dram"] for i in range(len(_OUTS)))
    return got[0]
```
